# Optimizing a Trainium2 kernel written in Bass

```python
import numpy as np
import jax
import jax.numpy as jnp

def _softmax(x, axis=-1):
    return jax.nn.softmax(x, axis=axis)

def _gelu(x):
    return jax.nn.gelu(x, approximate=True)

def _silu(x):
    return jax.nn.silu(x)

def _sigmoid(x):
    return jax.nn.sigmoid(x)

def _layernorm(x, axis=-1, eps=1e-05):
    m = jnp.mean(x, axis=axis, keepdims=True)
    v = jnp.var(x, axis=axis, keepdims=True)
    return (x - m) / jnp.sqrt(v + eps)

def _scatter_add(tgt, idx, src, axis=0):
    return tgt.at[idx].add(src)

def _segment_sum(src, seg, n):
    return jax.ops.segment_sum(src, seg, n)
kernel_name = 'mk_gnn_resnorm_d1_gnn_r8_726304'

def setup_inputs(seed: int=0):
    np.random.seed(seed)
    _w = jnp.asarray

    def _rec_inputs():
        import jax
        import jax.numpy as jnp
        _gk = jax.random.key(seed)
        x = -0.0001126 + 1 * jax.random.normal(jax.random.fold_in(_gk, 1), (6250, 256), jnp.float32)
        src = jax.random.randint(jax.random.fold_in(_gk, 2), (200000,), 0, 6250, jnp.int32)
        dst = jnp.minimum((6250 * jax.random.uniform(jax.random.fold_in(_gk, 3), (200000,)) ** 2.0).astype(jnp.int32), 49999)
        _o = jnp.argsort(dst, stable=True)
        src = src[_o]
        dst = dst[_o]
        return (x, src, dst)
    x, src, dst = _rec_inputs()

    def _L0_gnn_setup():
        import jax, jax.numpy as jnp
        import numpy as np
        N, E = (3750, 60000)
        D, H, DFF = (256, 8, 1024)
        HD = D // H

        def _layer_norm(x, g, b, eps=1e-05):
            mu = jnp.mean(x, axis=-1, keepdims=True)
            var = jnp.var(x, axis=-1, keepdims=True)
            return (x - mu) * jax.lax.rsqrt(var + eps) * g + b

        def _transformer_conv(x, src, dst, Wq, bq, Wk, bk, Wv, bv, Wskip, bskip):
            n = x.shape[0]
            q = (x @ Wq + bq).reshape(n, H, HD)
            k = (x @ Wk + bk).reshape(n, H, HD)
            v = (x @ Wv + bv).reshape(n, H, HD)
            qi = q[dst]
            kj = k[src]
            logits = jnp.sum(qi * kj, axis=-1) / np.sqrt(HD)
            m = jax.ops.segment_max(logits, dst, num_segments=n)
            m = jax.lax.stop_gradient(jnp.where(jnp.isfinite(m), m, 0.0))
            ex = jnp.exp(logits - m[dst])
            denom = jax.ops.segment_sum(ex, dst, num_segments=n)
            alpha = ex / (denom[dst] + 1e-16)
            msg = v[src] * alpha[..., None]
            out = jax.ops.segment_sum(msg, dst, num_segments=n).reshape(n, H * HD)
            return out + (x @ Wskip + bskip)
        key = jax.random.key(seed)
        ks = jax.random.split(key, 16)
        s = 0.02
        inp = {'node': jax.random.normal(ks[0], (N, D), dtype=jnp.float32), 'edge_index': jax.random.randint(ks[1], (2, E), 0, N, dtype=jnp.int64), 'Wq': jax.random.normal(ks[2], (D, H * HD), dtype=jnp.float32) * s, 'bq': jnp.zeros((H * HD,), dtype=jnp.float32), 'Wk': jax.random.normal(ks[3], (D, H * HD), dtype=jnp.float32) * s, 'bk': jnp.zeros((H * HD,), dtype=jnp.float32), 'Wv': jax.random.normal(ks[4], (D, H * HD), dtype=jnp.float32) * s, 'bv': jnp.zeros((H * HD,), dtype=jnp.float32), 'Wskip': jax.random.normal(ks[5], (D, H * HD), dtype=jnp.float32) * s, 'bskip': jnp.zeros((H * HD,), dtype=jnp.float32), 'Wo': jax.random.normal(ks[6], (H * HD, D), dtype=jnp.float32) * s, 'bo': jnp.zeros((D,), dtype=jnp.float32), 'W1': jax.random.normal(ks[7], (D, DFF), dtype=jnp.float32) * s, 'b1': jnp.zeros((DFF,), dtype=jnp.float32), 'W2': jax.random.normal(ks[8], (DFF, D), dtype=jnp.float32) * s, 'b2': jnp.zeros((D,), dtype=jnp.float32), 'g1': jnp.ones((D,), dtype=jnp.float32), 'be1': jnp.zeros((D,), dtype=jnp.float32), 'g2': jnp.ones((D,), dtype=jnp.float32), 'be2': jnp.zeros((D,), dtype=jnp.float32)}
        return inp
    _L0_gnn_all = _L0_gnn_setup()
    _L0_gnn_in = {k: v for k, v in _L0_gnn_all.items() if k in ('Wq', 'bq', 'Wk', 'bk', 'Wv', 'bv', 'Wskip', 'bskip', 'Wo', 'bo', 'W1', 'b1', 'W2', 'b2', 'g1', 'be1', 'g2', 'be2')}
    del _L0_gnn_all
    return {'x': x, 'src': src, 'dst': dst, 'L0_gnn_Wq': _L0_gnn_in['Wq'], 'L0_gnn_bq': _L0_gnn_in['bq'], 'L0_gnn_Wk': _L0_gnn_in['Wk'], 'L0_gnn_bk': _L0_gnn_in['bk'], 'L0_gnn_Wv': _L0_gnn_in['Wv'], 'L0_gnn_bv': _L0_gnn_in['bv'], 'L0_gnn_Wskip': _L0_gnn_in['Wskip'], 'L0_gnn_bskip': _L0_gnn_in['bskip'], 'L0_gnn_Wo': _L0_gnn_in['Wo'], 'L0_gnn_bo': _L0_gnn_in['bo'], 'L0_gnn_W1': _L0_gnn_in['W1'], 'L0_gnn_b1': _L0_gnn_in['b1'], 'L0_gnn_W2': _L0_gnn_in['W2'], 'L0_gnn_b2': _L0_gnn_in['b2'], 'L0_gnn_g1': _L0_gnn_in['g1'], 'L0_gnn_be1': _L0_gnn_in['be1'], 'L0_gnn_g2': _L0_gnn_in['g2'], 'L0_gnn_be2': _L0_gnn_in['be2']}

def reference(x, src, dst, L0_gnn_Wq, L0_gnn_bq, L0_gnn_Wk, L0_gnn_bk, L0_gnn_Wv, L0_gnn_bv, L0_gnn_Wskip, L0_gnn_bskip, L0_gnn_Wo, L0_gnn_bo, L0_gnn_W1, L0_gnn_b1, L0_gnn_W2, L0_gnn_b2, L0_gnn_g1, L0_gnn_be1, L0_gnn_g2, L0_gnn_be2):
    import jax
    import jax.numpy as jnp

    def _L0_gnn_ref(node, edge_index, Wq, bq, Wk, bk, Wv, bv, Wskip, bskip, Wo, bo, W1, b1, W2, b2, g1, be1, g2, be2):
        import jax, jax.numpy as jnp
        import numpy as np
        N, E = (3750, 60000)
        D, H, DFF = (256, 8, 1024)
        HD = D // H

        def _layer_norm(x, g, b, eps=1e-05):
            mu = jnp.mean(x, axis=-1, keepdims=True)
            var = jnp.var(x, axis=-1, keepdims=True)
            return (x - mu) * jax.lax.rsqrt(var + eps) * g + b

        def _transformer_conv(x, src, dst, Wq, bq, Wk, bk, Wv, bv, Wskip, bskip):
            n = x.shape[0]
            q = (x @ Wq + bq).reshape(n, H, HD)
            k = (x @ Wk + bk).reshape(n, H, HD)
            v = (x @ Wv + bv).reshape(n, H, HD)
            qi = q[dst]
            kj = k[src]
            logits = jnp.sum(qi * kj, axis=-1) / np.sqrt(HD)
            m = jax.ops.segment_max(logits, dst, num_segments=n)
            m = jax.lax.stop_gradient(jnp.where(jnp.isfinite(m), m, 0.0))
            ex = jnp.exp(logits - m[dst])
            denom = jax.ops.segment_sum(ex, dst, num_segments=n)
            alpha = ex / (denom[dst] + 1e-16)
            msg = v[src] * alpha[..., None]
            out = jax.ops.segment_sum(msg, dst, num_segments=n).reshape(n, H * HD)
            return out + (x @ Wskip + bskip)
        src, dst = (edge_index[0], edge_index[1])
        sa = _transformer_conv(node, src, dst, Wq, bq, Wk, bk, Wv, bv, Wskip, bskip)
        sa = sa @ Wo + bo
        x = _layer_norm(node + sa, g1, be1)
        ff = jax.nn.relu(x @ W1 + b1) @ W2 + b2
        return _layer_norm(x + ff, g2, be2)
    edge_index = jnp.stack([src, dst])
    x = _layernorm(x + _L0_gnn_ref(x, edge_index, L0_gnn_Wq, L0_gnn_bq, L0_gnn_Wk, L0_gnn_bk, L0_gnn_Wv, L0_gnn_bv, L0_gnn_Wskip, L0_gnn_bskip, L0_gnn_Wo, L0_gnn_bo, L0_gnn_W1, L0_gnn_b1, L0_gnn_W2, L0_gnn_b2, L0_gnn_g1, L0_gnn_be1, L0_gnn_g2, L0_gnn_be2), axis=-1)
    return x

_drawn_inputs = setup_inputs


def setup_inputs(seed=0):
    import zlib

    import numpy as np

    out = dict(_drawn_inputs(seed))
    spreads = {'L0_gnn_bq': (0.0, 0.8),
     'L0_gnn_bk': (0.0, 0.8),
     'L0_gnn_bv': (0.0, 0.502),
     'L0_gnn_bskip': (0.0, 0.461),
     'L0_gnn_bo': (0.0, 0.1),
     'L0_gnn_b1': (0.0, 0.376),
     'L0_gnn_b2': (0.0, 0.1),
     'L0_gnn_g1': (1.0, 0.2),
     'L0_gnn_be1': (0.0, 0.1),
     'L0_gnn_g2': (1.0, 0.2),
     'L0_gnn_be2': (0.0, 0.1)}
    factors = {'L0_gnn_Wq': 8.0, 'L0_gnn_Wk': 8.0, 'L0_gnn_Wv': 5.183}
    for name, (base, spread) in spreads.items():
        noise = np.random.default_rng([zlib.crc32(name.encode()), seed]).standard_normal(out[name].shape)
        drawn = base * np.exp(spread * noise) if base else spread * noise
        out[name] = jnp.asarray(drawn.astype(out[name].dtype))
    for name, factor in factors.items():
        out[name] = (out[name] * factor).astype(out[name].dtype)
    return out
```

```python
import numpy as np
import concourse.bass as bass
from concourse import mybir
from concourse.alu_op_type import AluOpType as ALU
from contextlib import ExitStack

F32 = mybir.dt.float32
I32 = mybir.dt.int32
ACT = mybir.ActivationFunctionType
AX = mybir.AxisListType
DVE = mybir.EngineType.DVE
PE = mybir.EngineType.PE

P = 128
N, D, E = 6250, 256, 200000
H, HD, FF = 8, 32, 1024
HC = HD + 1
KC = D // P
FC = FF // P
NT = -(-N // P)
TAIL = N - (NT - 1) * P
J = 4
GE = J * P
NG = -(-E // GE)
EP = NG * GE
NQ = -(-(NG + NT - 1) // 4) * 4
PC = -(-NQ // P)
NP = PC * P
PAD_DST = 1 << 20
BIG = 1e30
SCALE = float(1.0 / np.sqrt(HD))
NTAB = 3 * J


def at(start, count, size):
    return bass.ds(start * size, count * size)


def wait(eng, sem, n):
    if isinstance(n, int) and n <= 0:
        return
    eng.wait_ge(sem, n)


def hold(eng, sem, n, passed):
    if isinstance(n, int) and n <= 0:
        return
    eng.wait_ge(sem, n)
    eng.sem_inc(passed, 1)


def row_bcast(vec, n):
    return bass.AP(vec.tensor, 0, [[0, P], [1, n]])


def project(nc, x, w, kv_dram, Qs, ident, ident_ready):
    with ExitStack() as ctx:
        sb = lambda n, s, d=F32: ctx.enter_context(nc.sbuf_tensor(n, s, d))
        sem = lambda n: ctx.enter_context(nc.semaphore(n))
        wkv = sb("wkv", [P, KC, 2 * D])
        wq = sb("wq", [P, KC, D])
        bkv = sb("bkv", [P, 2 * D])
        bq = sb("bq", [P, D])
        xin = sb("xin", [P, 4, D])
        xT = sb("xT", [P, 2, KC, P])
        kvo = sb("kvo", [P, 4, 2 * D])
        psX = ctx.enter_context(nc.psum_tensor("psX", [P, 2, 512], F32))
        psKV = ctx.enter_context(nc.psum_tensor("psKV", [P, 2, 512], F32))
        psQp = ctx.enter_context(nc.psum_tensor("psQp", [P, 2, 512], F32))
        w_in = sem("w_in")
        b_in = sem("b_in")
        x_in = [sem(f"x_in{s}") for s in range(4)]
        xt_ps = sem("xt_ps")
        xt_sb = sem("xt_sb")
        proj_ps = sem("proj_ps")
        q_done = sem("q_done")
        kv_sb = sem("kv_sb")
        kv_out = [sem(f"kv_out{s}") for s in range(4)]

        def tiles(eng, step):
            for t in range(4):
                step(t, t, 0)
            with eng.Fori(4, NT - 4, 4) as i:
                for s in range(4):
                    step(i + s, s, i)
            step(NT - 1, (NT - 1) % 4, NT - 1)

        with nc.Block() as block:
            @block.sync
            def _(sp):
                def load(t, s, n4):
                    wait(sp, xt_ps, t - 3)
                    last = isinstance(t, int) and t == NT - 1
                    rows = TAIL if last else P
                    sp.dma_start(xin[0:rows, s, :], x[bass.ds(t * P, rows), :]).then_inc(x_in[s], 16)
                tiles(sp, load)

            @block.tensor
            def _(pe):
                pe.wait_ge(ident_ready, 2)
                pe.wait_ge(w_in, 3 * 16)
                def step(t, s, n4):
                    n = (n4 // 4) * 16 + 16 if isinstance(n4, int) else n4 * 4 + 16
                    pe.wait_ge(x_in[s], n)
                    wait(pe, xt_sb, t - 1)
                    for c in range(KC):
                        last = nc.tensor.transpose(psX[:, s % 2, c * P:(c + 1) * P], xin[:, s, c * P:(c + 1) * P], ident[:])
                    last.then_inc(xt_ps, 1)
                    pe.wait_ge(xt_sb, t + 1)
                    wait(pe, q_done, t - 1)
                    for c in range(KC):
                        nc.tensor.matmul(psKV[:, s % 2, :], xT[:, s % 2, c, :], wkv[:, c, :], start=c == 0, stop=c == KC - 1)
                    for c in range(KC):
                        last = nc.tensor.matmul(psQp[:, s % 2, 0:D], xT[:, s % 2, c, :], wq[:, c, :], start=c == 0, stop=c == KC - 1)
                    last.then_inc(proj_ps, 1)
                tiles(pe, step)

            @block.scalar
            def _(act):
                act.dma_start(wkv[:, :, 0:D], w["Wk"].rearrange("(c p) n -> p c n", p=P)).then_inc(w_in, 16)
                act.dma_start(wkv[:, :, D:2 * D], w["Wv"].rearrange("(c p) n -> p c n", p=P)).then_inc(w_in, 16)
                act.dma_start(wq[:], w["Wq"].rearrange("(c p) n -> p c n", p=P)).then_inc(w_in, 16)
                act.dma_start(bkv[:, 0:D], row_bcast(w["bk"], D)).then_inc(b_in, 16)
                act.dma_start(bkv[:, D:2 * D], row_bcast(w["bv"], D)).then_inc(b_in, 16)
                act.dma_start(bq[:], row_bcast(w["bq"], D)).then_inc(b_in, 16)

                def store(t, s, n4):
                    rows = TAIL if isinstance(t, int) and t == NT - 1 else P
                    act.wait_ge(kv_sb, t + 1)
                    act.dma_start(kv_dram[bass.ds(t * P, rows), :], kvo[0:rows, s, :]).then_inc(kv_out[s], 16)

                def step(t, s, n4):
                    act.wait_ge(xt_ps, t + 1)
                    wait(act, proj_ps, t - 1)
                    nc.scalar.copy(xT[:, s % 2].rearrange("p c n -> p (c n)"), psX[:, s % 2, 0:KC * P]).then_inc(xt_sb, 1)
                    if isinstance(t, int) and t == 0:
                        return
                    store(t - 1, (s - 1) % 4, n4)
                tiles(act, step)
                store(NT - 1, (NT - 1) % 4, 0)
                for s in range(4):
                    act.wait_ge(kv_out[s], 16 * len(range(s, NT, 4)))

            @block.vector
            def _(dve):
                dve.wait_ge(b_in, 3 * 16)

                def step(t, s, n4):
                    dve.wait_ge(proj_ps, t + 1)
                    if isinstance(n4, int):
                        if n4:
                            dve.wait_ge(kv_out[s], (n4 // 4) * 16)
                    else:
                        dve.wait_ge(kv_out[s], n4 * 4)
                    nc.vector.tensor_tensor(kvo[:, s, :], psKV[:, s % 2, :], bkv[:], ALU.add).then_inc(kv_sb, 1)
                    nc.vector.tensor_tensor(Qs[:, bass.ds(t, 1), :].rearrange("p a n -> p (a n)"), psQp[:, s % 2, 0:D], bq[:],
                                            ALU.add).then_inc(q_done, 1)
                tiles(dve, step)


def plan(nc, src, dst, srcp, dstp, tq_dram, TAB, IDX, trow, ident, ones, iota_row, pair_no):
    with ExitStack() as ctx:
        sb = lambda n, s, d=F32: ctx.enter_context(nc.sbuf_tensor(n, s, d))
        sem = lambda n: ctx.enter_context(nc.semaphore(n))
        padi = sb("padi", [1, 2, GE], I32)
        fl = sb("fl", [1, 2, NG], I32)
        flb = sb("flb", [1, 2, NG], I32)
        flf = sb("flf", [1, 2, NG])
        zrow = sb("zrow", [1, NG])
        cnt = sb("cnt", [1, NG])
        incl = sb("incl", [1, NG])
        start = sb("start", [1, 2, NG])
        cmpb = sb("cmpb", [P, NG])
        grp = sb("grp", [P, PC])
        shift = sb("shift", [P, PC])
        blk = sb("blk", [P, PC])
        blk128 = sb("blk128", [P, PC])
        grpi = sb("grpi", [P, PC], I32)
        blki = sb("blki", [P, PC], I32)
        rows = sb("rows", [P, 2, PC, GE], I32)
        dstf = sb("dstf", [P, GE])
        edge = sb("edge", [P, 4, GE])
        psB = ctx.enter_context(nc.psum_tensor("psB", [P, 2, 512], F32))
        psT = ctx.enter_context(nc.psum_tensor("psT", [P, 4, 512], F32))
        padded = sem("padded")
        pad_set = sem("pad_set")
        fl_in = sem("fl_in")
        v = sem("v")
        bc_ps = sem("bc_ps")
        rows_in = sem("rows_in")
        grp_ready = sem("grp_ready")
        tq_out = sem("tq_out")
        tq_in = sem("tq_in")
        edge_ready = sem("edge_ready")
        tr_ps = sem("tr_ps")
        tr_sb = sem("tr_sb")

        with nc.Block() as block:
            @block.sync
            def _(sp):
                sp.dma_start(srcp[0:E].rearrange("(a b) -> a b", a=16), src.rearrange("(a b) -> a b", a=16)).then_inc(padded, 16)
                sp.dma_start(dstp[0:E].rearrange("(a b) -> a b", a=16), dst.rearrange("(a b) -> a b", a=16)).then_inc(padded, 16)
                sp.wait_ge(pad_set, 2)
                sp.dma_start(srcp[E:EP][None, :], padi[0:1, 0, 0:EP - E]).then_inc(padded, 16)
                sp.dma_start(dstp[E:EP][None, :], padi[0:1, 1, 0:EP - E]).then_inc(padded, 16)
                with nc.allow_non_contiguous_dma("one element a group"):
                    sp.dma_start(fl[0:1, 0, :], bass.AP(dst.tensor, 0, [[0, 1], [GE, NG]])).then_inc(fl_in, 16)
                    sp.dma_start(fl[0:1, 1, 0:NG - 1], bass.AP(dst.tensor, GE - 1, [[0, 1], [GE, NG - 1]])).then_inc(fl_in, 16)
                    sp.dma_start(fl[0:1, 1, NG - 1:NG], bass.AP(dst.tensor, E - 1, [[0, 1], [1, 1]])).then_inc(fl_in, 16)
                    sp.wait_ge(grp_ready, 2)
                    sp.dma_start(tq_dram.rearrange("(c p) -> p c", p=P), blki[:]).then_inc(tq_out, 16)
                sp.wait_ge(tq_out, 16)
                sp.dma_start(trow[0:1, 0:NP], tq_dram[None, :]).then_inc(tq_in, 16)
                sp.wait_ge(tq_in, 16)

            @block.vector
            def _(dve):
                k = [0]

                def link(ins):
                    k[0] += 1
                    ins.then_inc(v, 1)
                    dve.wait_ge(v, k[0])
                nc.vector.memset(padi[:, 0, :], 0).then_inc(pad_set, 1)
                nc.vector.memset(padi[:, 1, :], PAD_DST).then_inc(pad_set, 1)
                nc.vector.memset(zrow[:], 0.0)
                dve.wait_ge(fl_in, 3 * 16)
                link(nc.vector.tensor_scalar(flb[:], fl[:], 7, None, ALU.arith_shift_right))
                link(nc.vector.tensor_copy(flf[:], flb[:]))
                link(nc.vector.tensor_tensor(cnt[:], flf[:, 1, :], flf[:, 0, :], ALU.subtract))
                link(nc.vector.tensor_scalar(cnt[:], cnt[:], 1.0, None, ALU.add))
                link(nc.vector.tensor_tensor_scan(incl[:], zrow[:], cnt[:], 0.0, ALU.add, ALU.add))
                link(nc.vector.tensor_tensor(start[:, 0, :], incl[:], cnt[:], ALU.subtract))
                nc.vector.tensor_tensor(start[:, 1, :], flf[:, 0, :], start[:, 0, :], ALU.subtract).then_inc(edge_ready, 1)
                dve.wait_ge(bc_ps, 1)
                for c in range(PC):
                    link(nc.vector.tensor_scalar(cmpb[:], psB[:, 0, 0:NG], pair_no[:, c:c + 1], None, ALU.is_le))
                    link(nc.vector.tensor_reduce(grp[:, c:c + 1], cmpb[:], AX.X, ALU.add))
                link(nc.vector.tensor_scalar(grp[:], grp[:], -1.0, None, ALU.add))
                nc.vector.tensor_copy(grpi[:], grp[:]).then_inc(grp_ready, 1)
                for c in range(PC):
                    link(nc.vector.tensor_scalar(cmpb[:], iota_row[:, 0:NG], grp[:, c:c + 1], None, ALU.is_equal))
                    link(nc.vector.tensor_tensor(cmpb[:], psB[:, 1, 0:NG], cmpb[:], ALU.mult))
                    link(nc.vector.tensor_reduce(shift[:, c:c + 1], cmpb[:], AX.X, ALU.add))
                link(nc.vector.tensor_tensor(blk[:], shift[:], pair_no[:], ALU.add))
                link(nc.vector.tensor_scalar(blk128[:], blk[:], float(P), None, ALU.mult))
                link(nc.vector.tensor_scalar(blk[:], blk[:], float(NT - 1), None, ALU.min))
                nc.vector.tensor_copy(blki[:], blk[:]).then_inc(grp_ready, 1)
                for c in range(PC):
                    dve.wait_ge(rows_in, 32 * (c + 1))
                    link(nc.vector.tensor_copy(dstf[:], rows[:, 1, c, :]))
                    nc.vector.tensor_copy(edge[:, 3, :], rows[:, 0, c, :])
                    nc.vector.tensor_scalar(edge[:, 0, :], dstf[:], blk128[:, c:c + 1], None, ALU.subtract)
                    link(nc.vector.tensor_tensor(edge[:, 1, 0:GE - 1], dstf[:, 1:GE], dstf[:, 0:GE - 1], ALU.not_equal))
                    link(nc.vector.tensor_scalar(edge[:, 2, 1:GE], edge[:, 1, 0:GE - 1], -BIG, None, ALU.mult))
                    link(nc.vector.memset(edge[:, 1, P - 1:GE:P], 1.0))
                    nc.vector.memset(edge[:, 2, 0:GE:P], -BIG).then_inc(edge_ready, 1)
                    for a in range(4):
                        dve.wait_ge(tr_ps, c * 4 + a + 1)
                        got = psT[:, a, :].rearrange("p (j g) -> p g j", j=J)
                        if a < 3:
                            out = TAB[:, c * P:(c + 1) * P, a * J:(a + 1) * J]
                        else:
                            out = IDX[:, c * P:(c + 1) * P, :]
                        nc.vector.tensor_copy(out, got).then_inc(tr_sb, 1)

            @block.gpsimd
            def _(pool):
                pool.wait_ge(padded, 4 * 16)
                pool.wait_ge(grp_ready, 1)
                for c in range(PC):
                    for k, lst in ((0, srcp), (1, dstp)):
                        if c or k:
                            pool.wait_ge(rows_in, 16 * (2 * c + k))
                        nc.gpsimd.indirect_dma_start(
                            rows[:, k, c, :], None, lst.rearrange("(a b) -> a b", b=GE),
                            bass.IndirectOffsetOnAxis(ap=grpi[:, c:c + 1], axis=0)).then_inc(rows_in, 16)

            @block.tensor
            def _(pe):
                pe.wait_ge(edge_ready, 1)
                for k in range(2):
                    last = nc.tensor.matmul(psB[:, k, 0:NG], ones[:], start[:, k, :], start=True, stop=True)
                last.then_inc(bc_ps, 1)
                for c in range(PC):
                    pe.wait_ge(edge_ready, 2 + c)
                    for a in range(4):
                        n = c * 4 + a
                        if n >= 4:
                            pe.wait_ge(tr_sb, n - 3)
                        for j in range(J):
                            last = nc.tensor.transpose(psT[:, a, j * P:(j + 1) * P], edge[:, a, j * P:(j + 1) * P], ident[:])
                        last.then_inc(tr_ps, 1)


def edges(nc, kv_dram, Qs, acc, mx, TAB, IDX, trow, ident, iota_row):
    with ExitStack() as ctx:
        sb = lambda n, s, d=F32: ctx.enter_context(nc.sbuf_tensor(n, s, d))
        ps = lambda n, s: ctx.enter_context(nc.psum_tensor(n, s, F32))
        sem = lambda n: ctx.enter_context(nc.semaphore(n))
        R = 4
        kv = sb("kv", [P, R, J, 2 * D])
        cols = sb("cols", [P, R, 2 * J])
        brkb = sb("brkb", [P, R, J, H])
        idx = sb("idx", [P, R, J], I32)
        oh = sb("oh", [P, R, J, P])
        ohT = sb("ohT", [P, R, J, P])
        prod = sb("prod", [P, J * D])
        lg = sb("lg", [P, 2, J * H])
        msk = sb("msk", [J * H, 2, P])
        run = sb("run", [J * H, 2, P])
        last9 = sb("last9", [P, R, J, H + 1])
        absent = sb("absent", [P, J])
        cand = sb("cand", [P, J, H])
        qmax = sb("qmax", [P, H])
        mnew = sb("mnew", [P, 2, H])
        md = sb("md", [P, R, H])
        arg = sb("arg", [P, 2, J * H])
        cf = sb("cf", [P, R, H])
        msg = sb("msg", [P, 2, J, H, HC])
        psQ = ps("psQ", [P, J * D])
        psHT = ps("psHT", [P, 512])
        psO = ps("psO", [P, 2, 512])
        psL = ps("psL", [P, 512])
        psM = ps("psM", [P, 512])
        psS = ps("psS", [P, 512])
        sLT = psL[0:J * H, 0:P]
        sMK = psM[0:J * H, 0:P]
        sST = psS[:, 256:256 + J * H]
        sNM = psS[:, 288:288 + J * (H + 1)]
        sME = psS[:, 336:336 + J * H]

        names = ("cols_ready idx_ready oh_ready oht_ps oht_sb q_half l_ready prod_a mask_ps mask_sb lt_ps scan_done st_ps sl_ready "
                 "nmax_ps m_ready mexp_ps arg_ready p_ready c_ready msg_ready seg_ps acc_scaled acc_done absent_ok cand_ok qmax_ok mnew_ok passed").split()
        S = {n: sem(n) for n in names}
        kv_in = [sem(f"kv_in{s}") for s in range(R)]
        init = sem("init")

        def steps(eng, step, lead, load=None):
            for i in range(4):
                step(i, i, load(i) if load else None)
            with eng.Fori(4, NQ - 3, 4) as i:
                ts = load(i) if load else None
                for s in range(4):
                    step(i + s, s, ts)
            for i in range(NQ, NQ + lead):
                step(i, i % 4, load(i) if load else None)

        def has(i, k):
            return not isinstance(i, int) or 0 <= i + k < NQ

        def group(i, slot):
            return (i // 4 + 1) * 64 if isinstance(i, int) else (i - slot) * 16 + 64

        with nc.Block() as block:
            @block.gpsimd
            def _(pool):
                def step(i, s, _):
                    hold(pool, S["idx_ready"], i + 1, S["passed"])
                    hold(pool, S["msg_ready"], i - R + 1, S["passed"])
                    for j in range(J):
                        nc.gpsimd.indirect_dma_start(
                            kv[:, s, j, :], None, kv_dram[:, :],
                            bass.IndirectOffsetOnAxis(ap=idx[:, s, j:j + 1], axis=0)).then_inc(kv_in[s], 16)
                steps(pool, step, 0)

            @block.scalar
            def _(act):
                def columns(q, s):
                    ent = TAB[:, bass.ds(q, 1), :]
                    nc.scalar.copy(cols[:, s, :], ent[:, :, 0:2 * J].rearrange("p a n -> p (a n)"))
                    nc.scalar.copy(last9[:, s, :, H:H + 1], ent[:, :, J:2 * J].rearrange("p a n -> p n a"))
                    nc.scalar.copy(brkb[:, s], ent[:, :, 2 * J:3 * J].rearrange("p a n -> p n a").to_broadcast([P, J, H])).then_inc(S["cols_ready"], 1)
                    nc.scalar.copy(idx[:, s, :], IDX[:, bass.ds(q, 1), :].rearrange("p a n -> p (a n)")).then_inc(S["idx_ready"], 1)

                def step(i, s, _):
                    if has(i, 0):
                        act.wait_ge(S["mask_ps"], i + 1)
                        wait(act, S["scan_done"], i - 1)
                        nc.scalar.copy(msk[:, s % 2, :], sMK).then_inc(S["mask_sb"], 1)
                    if has(i, 1):
                        act.wait_ge(S["oht_ps"], i + 2)
                        nc.scalar.copy(ohT[:, (s + 1) % 4].rearrange("p j n -> p (j n)"), psHT[:]).then_inc(S["oht_sb"], 1)
                    if has(i, -1):
                        act.wait_ge(S["m_ready"], i)
                        nc.scalar.activation(cf[:, (s - 1) % 4, :], md[:, (s - 1) % 4, :], ACT.Exp, scale=SCALE).then_inc(S["c_ready"], 1)
                        act.wait_ge(S["arg_ready"], i)
                        wait(act, S["seg_ps"], i - 2)
                        nc.scalar.activation(msg[:, (s - 1) % 2, :, :, HD:HC], arg[:, (s - 1) % 2, :].rearrange("p (j h a) -> p j h a", j=J, a=1),
                                             ACT.Exp, scale=SCALE).then_inc(S["p_ready"], 1)
                    if has(i, 3) and has(i, -1):
                        columns(i + 3, (s + 3) % 4)
                act.wait_ge(init, 1)
                for q in range(3):
                    columns(q, q)
                act.wait_ge(S["oht_ps"], 1)
                nc.scalar.copy(ohT[:, 0].rearrange("p j n -> p (j n)"), psHT[:]).then_inc(S["oht_sb"], 1)
                columns(3, 3)
                steps(act, step, 1)

            @block.tensor
            def _(pe):
                def onehot_T(q, s):
                    pe.wait_ge(S["oh_ready"], q + 1)
                    wait(pe, S["oht_sb"], q)
                    for j in range(J):
                        last = nc.tensor.transpose(psHT[:, j * P:(j + 1) * P], oh[:, s, j, :], ident[:])
                    last.then_inc(S["oht_ps"], 1)

                def expand_q(q, s, t, half):
                    if half == 0:
                        pe.wait_ge(S["oht_sb"], q + 1)
                    wait(pe, S["prod_a"], 2 * q - 1 + half)
                    for j in (2 * half, 2 * half + 1):
                        last = nc.tensor.matmul(psQ[:, j * D:(j + 1) * D], ohT[:, s, j, :],
                                                Qs[:, bass.ds(t, 1), :].rearrange("p a n -> p (a n)"), start=True, stop=True)
                    last.then_inc(S["q_half"], 1)

                def load(i):
                    _, ts = nc.values_load_multi_w_load_instructions(trow[0:1, bass.ds(i + 1, 4)] if not isinstance(i, int) else trow[0:1, i + 1:i + 5],
                                                                     engines=[PE], min_val=0, max_val=NT - 1)
                    return ts

                def step(i, s, ts):
                    t = None if ts is None else ts[s if not isinstance(i, int) else 0]
                    p, s1, s2 = (s - 1) % 4, (s + 1) % 4, (s - 2) % 4
                    if has(i, -1):
                        pe.wait_ge(S["l_ready"], i)
                        nc.tensor.transpose(sLT, lg[:, p % 2, :], ident[:]).then_inc(S["lt_ps"], 1)
                    if has(i, 0):
                        wait(pe, S["mask_sb"], i)
                        nc.tensor.matmul(sMK, brkb[:, s].rearrange("p j h -> p (j h)"), ident[:], start=True, stop=True).then_inc(S["mask_ps"], 1)
                    if has(i, 1):
                        onehot_T(i + 1, s1)
                    if has(i, -1):
                        hold(pe, S["scan_done"], i, S["passed"])
                        nc.tensor.transpose(sST, run[:, p % 2, :], ident[0:J * H, 0:J * H]).then_inc(S["st_ps"], 1)
                    if has(i, 1):
                        expand_q(i + 1, s1, t, 0)
                    if has(i, -1):
                        pe.wait_ge(S["sl_ready"], i)
                        for j in range(J):
                            last = nc.tensor.matmul(sNM[:, j * (H + 1):(j + 1) * (H + 1)], oh[:, p, j, :], last9[:, p, j, :], start=True, stop=True)
                        last.then_inc(S["nmax_ps"], 1)
                    if has(i, 1):
                        expand_q(i + 1, s1, t, 1)
                    if has(i, -1):
                        pe.wait_ge(S["m_ready"], i)
                        for j in range(J):
                            last = nc.tensor.matmul(sME[:, j * H:(j + 1) * H], ohT[:, p, j, :], mnew[:, p % 2, :], start=True, stop=True)
                        last.then_inc(S["mexp_ps"], 1)
                    if has(i, -2):
                        pe.wait_ge(S["msg_ready"], i - 1)
                        wait(pe, S["acc_done"], i - 3)
                        for j in range(J):
                            last = nc.tensor.matmul(psO[:, s2 % 2, 0:H * HC], oh[:, s2, j, :], msg[:, s2 % 2, j].rearrange("p h c -> p (h c)"),
                                                    start=j == 0, stop=j == J - 1)
                        last.then_inc(S["seg_ps"], 1)
                onehot_T(0, 0)
                _, t0 = nc.values_load_multi_w_load_instructions(trow[0:1, 0:1], engines=[PE], min_val=0, max_val=NT - 1)
                expand_q(0, 0, t0[0], 0)
                expand_q(0, 0, t0[0], 1)
                steps(pe, step, 2, load)

            @block.vector
            def _(dve):
                def onehot(q, s):
                    dve.wait_ge(S["cols_ready"], q + 1)
                    wait(dve, S["seg_ps"], q - 3)
                    for j in range(J):
                        last = nc.vector.tensor_scalar(oh[:, s, j, :], iota_row[:, 0:P], cols[:, s, j:j + 1], None, ALU.is_equal)
                    last.then_inc(S["oh_ready"], 1)

                def load(i):
                    if isinstance(i, int):
                        lo = max(i - 3, 0)
                        n = min(i, NQ + 3) - lo + 1
                        _, ts = nc.values_load_multi_w_load_instructions(trow[0:1, lo:lo + 4], engines=[DVE], min_val=0, max_val=NT - 1)
                        return {k - i: ts[k - lo] for k in range(lo, i) if k < NQ}
                    _, ts = nc.values_load_multi_w_load_instructions(trow[0:1, bass.ds(i - 3, 6)], engines=[DVE], min_val=0, max_val=NT - 1)
                    return {k - 3: ts[k] for k in range(6)}

                def step(i, s, ts):
                    off = 0 if isinstance(i, int) else s
                    p, s1, s2, s3 = (s - 1) % 4, (s + 1) % 4, (s - 2) % 4, (s - 3) % 4
                    if has(i, 0):
                        dve.wait_ge(kv_in[s], group(i, s))
                        dve.wait_ge(S["q_half"], i * 2 + 1)
                        wait(dve, S["l_ready"], i)
                        nc.vector.tensor_tensor(prod[:, 0:2 * D].rearrange("p (j n) -> p j n", j=2), psQ[:, 0:2 * D].rearrange("p (j n) -> p j n", j=2),
                                                kv[:, s, 0:2, 0:D], ALU.mult).then_inc(S["prod_a"], 1)
                    if has(i, -1):
                        dve.wait_ge(S["lt_ps"], i)
                        dve.wait_ge(S["mask_sb"], i)
                        nc.vector.tensor_tensor_scan(run[:, p % 2, :], msk[:, p % 2, :], sLT, -BIG, ALU.add, ALU.max).then_inc(S["scan_done"], 1)
                    if has(i, 0):
                        dve.wait_ge(S["q_half"], i * 2 + 2)
                        nc.vector.tensor_tensor(prod[:, 2 * D:4 * D].rearrange("p (j n) -> p j n", j=2), psQ[:, 2 * D:4 * D].rearrange("p (j n) -> p j n", j=2),
                                                kv[:, s, 2:4, 0:D], ALU.mult).then_inc(S["prod_a"], 1)
                    if has(i, 1):
                        onehot(i + 1, s1)
                    if has(i, -1):
                        dve.wait_ge(S["st_ps"], i)
                        nc.vector.tensor_tensor(last9[:, p, :, 0:H], sST.rearrange("p (j h) -> p j h", j=J),
                                                cols[:, p, J:2 * J].rearrange("p (j a) -> p j a", a=1).to_broadcast([P, J, H]), ALU.mult).then_inc(S["sl_ready"], 1)
                    if has(i, 0):
                        dve.wait_ge(S["prod_a"], i * 2 + 2)
                        nc.vector.tensor_reduce(lg[:, s % 2, :], prod[:].rearrange("p (g c) -> p g c", c=HD), AX.X, ALU.add).then_inc(S["l_ready"], 1)
                    if has(i, -1):
                        t = ts[off - 1]
                        mcur = mx[:, bass.ds(t, 1), :].rearrange("p a h -> p (a h)")
                        dve.wait_ge(S["nmax_ps"], i)
                        nm = sNM.rearrange("p (j h) -> p j h", j=J)
                        nc.vector.tensor_scalar(absent[:].rearrange("p (j a) -> p j a", a=1), nm[:, :, H:H + 1], BIG, -BIG, ALU.mult, ALU.add).then_inc(S["absent_ok"], 1)
                        dve.wait_ge(S["absent_ok"], i)
                        nc.vector.tensor_tensor(cand[:], nm[:, :, 0:H], absent[:].rearrange("p (j a) -> p j a", a=1).to_broadcast([P, J, H]), ALU.add).then_inc(S["cand_ok"], 1)
                        dve.wait_ge(S["cand_ok"], i)
                        nc.vector.tensor_reduce(qmax[:], cand[:].rearrange("p j h -> p h j"), AX.X, ALU.max).then_inc(S["qmax_ok"], 1)
                        dve.wait_ge(S["qmax_ok"], i)
                        nc.vector.tensor_tensor(mnew[:, p % 2, :], mcur, qmax[:], ALU.max).then_inc(S["mnew_ok"], 1)
                        dve.wait_ge(S["mnew_ok"], i)
                        nc.vector.tensor_tensor(md[:, p, :], mcur, mnew[:, p % 2, :], ALU.subtract).then_inc(S["m_ready"], 1)
                        dve.wait_ge(S["m_ready"], i)
                        nc.vector.tensor_tensor(mcur, mnew[:, p % 2, :], mnew[:, p % 2, :], ALU.max)
                    if has(i, -2):
                        dve.wait_ge(S["p_ready"], i - 1)
                        for half in (0, 1):
                            js = slice(2 * half, 2 * half + 2)
                            m = nc.vector.tensor_tensor(msg[:, s2 % 2, js, :, 0:HD], kv[:, s2, js, D:2 * D].rearrange("p j (h c) -> p j h c", h=H),
                                                        msg[:, s2 % 2, js, :, HD:HC].to_broadcast([P, 2, H, HD]), ALU.mult)
                            if half == 0 and has(i, -1):
                                dve.wait_ge(S["mexp_ps"], i)
                                nc.vector.tensor_tensor(arg[:, p % 2, :], lg[:, p % 2, :], sME, ALU.subtract).then_inc(S["arg_ready"], 1)
                        m.then_inc(S["msg_ready"], 1)
                    elif has(i, -1):
                        dve.wait_ge(S["mexp_ps"], i)
                        nc.vector.tensor_tensor(arg[:, p % 2, :], lg[:, p % 2, :], sME, ALU.subtract).then_inc(S["arg_ready"], 1)
                    if has(i, -3):
                        ac = acc[:, bass.ds(ts[off - 3], 1)].rearrange("p a h c -> p (a h) c")
                        dve.wait_ge(S["c_ready"], i - 2)
                        wait(dve, S["acc_done"], i - 3)
                        nc.vector.tensor_tensor(ac, ac, cf[:, s3, :].rearrange("p (h a) -> p h a", a=1).to_broadcast([P, H, HC]), ALU.mult).then_inc(S["acc_scaled"], 1)
                        dve.wait_ge(S["acc_scaled"], i - 2)
                        dve.wait_ge(S["seg_ps"], i - 2)
                        nc.vector.tensor_tensor(ac, ac, psO[:, s3 % 2, 0:H * HC].rearrange("p (h c) -> p h c", h=H), ALU.add).then_inc(S["acc_done"], 1)

                nc.vector.memset(acc[:].rearrange("p a h c -> p (a h c)"), 0.0)
                nc.vector.memset(mx[:], -BIG).then_inc(init, 1)
                dve.wait_ge(init, 1)
                onehot(0, 0)
                steps(dve, step, 3, load)
                dve.wait_ge(S["acc_done"], NQ)


def nodes(nc, x, w, out, acc, ident):
    with ExitStack() as ctx:
        sb = lambda n, s, d=F32: ctx.enter_context(nc.sbuf_tensor(n, s, d))
        ps = lambda n, s: ctx.enter_context(nc.psum_tensor(n, s, F32))
        sem = lambda n: ctx.enter_context(nc.semaphore(n))
        wsk = sb("wsk", [P, KC, D])
        wo = sb("wo", [P, KC, D])
        w1 = sb("w1", [P, KC, FF])
        w2 = sb("w2", [P, FC, D])
        rows = {n: sb(f"r_{n}", [P, D]) for n in ("bskip", "bo", "b2", "g1", "be1", "g2", "be2")}
        b1c = sb("b1c", [P, FC])
        xin = sb("nx", [P, 4, D])
        xT = sb("nxT", [P, KC * P])
        saT = sb("saT", [P, KC * P])
        x1T = sb("x1T", [P, KC * P])
        den = sb("den", [P, H])
        att = sb("att", [P, D])
        sa = sb("sa", [P, D])
        y = sb("y", [P, D])
        x1 = sb("x1", [P, D])
        hT = sb("hT", [P, FC, P])
        st = sb("st", [P, 6])
        ag = sb("ag", [P, 2])
        sd = sb("sd", [P, 1])
        rs = sb("rs", [P, 1])
        ob = sb("ob", [P, 2, D])
        eps = sb("eps", [P, 1])
        pX = ps("pX", [P, 512])
        pS = ps("pS", [P, 512])
        pA = ps("pA", [P, 512])
        pB = ps("pB", [P, 512])
        pH = ps("pH", [P, 2, 512])
        pF = ps("pF", [P, 512])
        pC = ps("pC", [P, 512])
        w_in = sem("nw_in")
        x_in = [sem(f"nx_in{s}") for s in range(4)]
        out_done = [sem(f"out_done{s}") for s in range(2)]
        names = "xt_ps xt_sb skip_ps sa_ready sat_ps sat_sb wo_ps x1_ready x1t_ps x1t_sb h_ps h_sb f_ps stat sd_ready o_ready v eps_ok passed".split()
        S = {n: sem("n_" + n) for n in names}

        def tiles(eng, step, group=4):
            for t in range(4):
                step(t, t, 0)
            with eng.Fori(4, NT - 4, 4) as i:
                for s in range(4):
                    step(i + s, s, i)
            step(NT - 1, (NT - 1) % 4, NT - 1)

        with nc.Block() as block:
            @block.sync
            def _(sp):
                for t, d in ((wsk, "Wskip"), (wo, "Wo"), (w1, "W1")):
                    sp.dma_start(t[:], w[d].rearrange("(c p) n -> p c n", p=P)).then_inc(w_in, 16)
                sp.dma_start(w2[:], w["W2"].rearrange("(c p) n -> p c n", p=P)).then_inc(w_in, 16)
                for n, t in rows.items():
                    sp.dma_start(t[:], row_bcast(w[n], D)).then_inc(w_in, 16)
                with nc.allow_non_contiguous_dma("a bias by partitions"):
                    sp.dma_start(b1c[:], w["b1"].rearrange("(c p) -> p c", p=P)).then_inc(w_in, 16)

                def load(t, s, n4):
                    wait(sp, S["o_ready"], t - 3)
                    r = TAIL if isinstance(t, int) and t == NT - 1 else P
                    sp.dma_start(xin[0:r, s, :], x[bass.ds(t * P, r), :]).then_inc(x_in[s], 16)
                tiles(sp, load)

            @block.tensor
            def _(pe):
                pe.wait_ge(w_in, 12 * 16)

                def turn(dst, src_, ready, n, out_):
                    pe.wait_ge(ready, n)
                    for c in range(KC):
                        last = nc.tensor.transpose(dst[:, c * P:(c + 1) * P], src_[:, c * P:(c + 1) * P], ident[:])
                    last.then_inc(out_, 1)

                def step(t, s, n4):
                    n = (n4 // 4) * 16 + 16 if isinstance(n4, int) else n4 * 4 + 16
                    turn(pX, xin[:, s, :], x_in[s], n, S["xt_ps"])
                    pe.wait_ge(S["xt_sb"], t + 1)
                    for c in range(KC):
                        last = nc.tensor.matmul(pS[:, 0:D], xT[:, c * P:(c + 1) * P], wsk[:, c, :], start=c == 0, stop=c == KC - 1)
                    last.then_inc(S["skip_ps"], 1)
                    turn(pA, sa[:], S["sa_ready"], t + 1, S["sat_ps"])
                    pe.wait_ge(S["sat_sb"], t + 1)
                    for c in range(KC):
                        last = nc.tensor.matmul(pB[:, 0:D], saT[:, c * P:(c + 1) * P], wo[:, c, :], start=c == 0, stop=c == KC - 1)
                    last.then_inc(S["wo_ps"], 1)
                    turn(pC, x1[:], S["x1_ready"], t + 1, S["x1t_ps"])
                    pe.wait_ge(S["x1t_sb"], t + 1)
                    for f in range(FC):
                        for c in range(KC):
                            last = nc.tensor.matmul(pH[:, f // 4, (f % 4) * P:(f % 4 + 1) * P], w1[:, c, f * P:(f + 1) * P], x1T[:, c * P:(c + 1) * P],
                                                    start=c == 0, stop=c == KC - 1)
                        if f % 4 == 3:
                            last.then_inc(S["h_ps"], 1)
                    for f in range(FC):
                        pe.wait_ge(S["h_sb"], t * FC + f + 1)
                        last = nc.tensor.matmul(pF[:, 0:D], hT[:, f, :], w2[:, f, :], start=f == 0, stop=f == FC - 1)
                    last.then_inc(S["f_ps"], 1)
                tiles(pe, step)

            @block.scalar
            def _(act):
                act.wait_ge(S["eps_ok"], 1)
                act.wait_ge(w_in, 12 * 16)

                def root(n):
                    act.wait_ge(S["stat"], n)
                    nc.scalar.activation(sd[:], ag[:, 1:2], ACT.Sqrt, bias=eps[:]).then_inc(S["sd_ready"], 1)

                def step(t, s, n4):
                    act.wait_ge(S["xt_ps"], t + 1)
                    nc.scalar.copy(xT[:], pX[:, 0:KC * P]).then_inc(S["xt_sb"], 1)
                    act.wait_ge(S["sat_ps"], t + 1)
                    nc.scalar.copy(saT[:], pA[:, 0:KC * P]).then_inc(S["sat_sb"], 1)
                    root(t * 3 + 1)
                    act.wait_ge(S["x1t_ps"], t + 1)
                    nc.scalar.copy(x1T[:], pC[:, 0:KC * P]).then_inc(S["x1t_sb"], 1)
                    for f in range(FC):
                        act.wait_ge(S["h_ps"], t * 2 + f // 4 + 1)
                        nc.scalar.activation(hT[:, f, :], pH[:, f // 4, (f % 4) * P:(f % 4 + 1) * P], ACT.Relu, bias=b1c[:, f:f + 1]).then_inc(S["h_sb"], 1)
                    root(t * 3 + 2)
                    root(t * 3 + 3)
                tiles(act, step)

            @block.gpsimd
            def _(pool):
                def step(t, s, n4):
                    pool.wait_ge(S["o_ready"], t + 1)
                    r = TAIL if isinstance(t, int) and t == NT - 1 else P
                    pool.dma_start(out[bass.ds(t * P, r), :], ob[0:r, s % 2, :]).then_inc(out_done[s % 2], 16)
                tiles(pool, step)
                pool.wait_ge(out_done[0], 16 * len(range(0, NT, 2)))
                pool.wait_ge(out_done[1], 16 * len(range(1, NT, 2)))

            @block.vector
            def _(dve):
                nc.vector.memset(eps[:], 1e-5).then_inc(S["eps_ok"], 1)
                dve.wait_ge(w_in, 12 * 16)
                PER = 20

                def step(t, s, n4):
                    k = [0]

                    def link(ins):
                        k[0] += 1
                        ins.then_inc(S["v"], 1)
                        dve.wait_ge(S["v"], t * PER + k[0])

                    def norm(n, out_, in_):
                        link(nc.vector.bn_stats(st[:], in_))
                        dve.sem_inc(S["passed"], 1)
                        nc.vector.bn_aggr(ag[:], st[:]).then_inc(S["stat"], 1)
                        dve.wait_ge(S["sd_ready"], n)
                        link(nc.vector.reciprocal(rs[:], sd[:]))
                        return nc.vector.tensor_scalar(out_, in_, ag[:, 0:1], rs[:, 0:1], ALU.subtract, ALU.mult)
                    ac = acc[:, bass.ds(t, 1)].rearrange("p a h c -> p (a h) c")
                    link(nc.vector.tensor_scalar(den[:].rearrange("p (h a) -> p h a", a=1), ac[:, :, HD:HC], 1e-16, None, ALU.add))
                    link(nc.vector.reciprocal(den[:], den[:]))
                    link(nc.vector.tensor_tensor(att[:].rearrange("p (h c) -> p h c", h=H), ac[:, :, 0:HD],
                                                 den[:].rearrange("p (h a) -> p h a", a=1).to_broadcast([P, H, HD]), ALU.mult))
                    link(nc.vector.tensor_tensor(att[:], att[:], rows["bskip"][:], ALU.add))
                    dve.wait_ge(S["skip_ps"], t + 1)
                    nc.vector.tensor_tensor(sa[:], att[:], pS[:, 0:D], ALU.add).then_inc(S["sa_ready"], 1)
                    link(nc.vector.tensor_tensor(y[:], xin[:, s, :], rows["bo"][:], ALU.add))
                    dve.wait_ge(S["wo_ps"], t + 1)
                    link(nc.vector.tensor_tensor(y[:], y[:], pB[:, 0:D], ALU.add))
                    link(norm(t * 3 + 1, x1[:], y[:]))
                    link(nc.vector.tensor_tensor(x1[:], x1[:], rows["g1"][:], ALU.mult))
                    nc.vector.tensor_tensor(x1[:], x1[:], rows["be1"][:], ALU.add).then_inc(S["x1_ready"], 1)
                    dve.wait_ge(S["x1_ready"], t + 1)
                    link(nc.vector.tensor_tensor(y[:], x1[:], rows["b2"][:], ALU.add))
                    dve.wait_ge(S["f_ps"], t + 1)
                    link(nc.vector.tensor_tensor(y[:], y[:], pF[:, 0:D], ALU.add))
                    link(norm(t * 3 + 2, y[:], y[:]))
                    link(nc.vector.tensor_tensor(y[:], y[:], rows["g2"][:], ALU.mult))
                    link(nc.vector.tensor_tensor(y[:], y[:], rows["be2"][:], ALU.add))
                    link(nc.vector.tensor_tensor(y[:], y[:], xin[:, s, :], ALU.add))
                    if isinstance(t, int):
                        wait(dve, out_done[s % 2], (t // 2) * 16)
                    else:
                        dve.wait_ge(out_done[s % 2], (n4 + (s - s % 2)) * 8)
                    norm(t * 3 + 3, ob[:, s % 2, :], y[:]).then_inc(S["o_ready"], 1)
                    assert k[0] == PER, k[0]
                tiles(dve, step)


def gnn_program(nc, x, src, dst, w, out):
    kv_dram = nc.dram_tensor("kv_table", (N, 2 * D), F32, kind="Internal").ap()
    srcp = nc.dram_tensor("src_padded", (EP,), I32, kind="Internal").ap()
    dstp = nc.dram_tensor("dst_padded", (EP,), I32, kind="Internal").ap()
    tq_dram = nc.dram_tensor("pair_block", (NP,), I32, kind="Internal").ap()
    with ExitStack() as ctx:
        sb = lambda n, s, d=F32: ctx.enter_context(nc.sbuf_tensor(n, s, d))
        ident = sb("ident", [P, P])
        ones = sb("ones", [1, P])
        iota_row = sb("iota_row", [P, 512])
        pair_no = sb("pair_no", [P, PC])
        acc = sb("acc", [P, NT, H, HC])
        ready = ctx.enter_context(nc.semaphore("const_ready"))
        with ExitStack() as c2:
            sb2 = lambda n, s, d=F32: c2.enter_context(nc.sbuf_tensor(n, s, d))
            Qs = sb2("Qs", [P, NT, D])
            mx = sb2("mx", [P, NT, H])
            TAB = sb2("TAB", [P, NP, NTAB])
            IDX = sb2("IDX", [P, NP, J], I32)
            trow = sb2("trow", [1, NP], I32)
            with nc.Block() as block:
                @block.gpsimd
                def _(pool):
                    nc.gpsimd.memset(ones[:], 1.0)
                    nc.gpsimd.memset(ident[:], 0.0).then_inc(ready, 1)
                    pool.wait_ge(ready, 1)
                    nc.gpsimd.affine_select(ident[:], ident[:], [[-1, P]], ALU.not_equal, 1.0, base=0, channel_multiplier=1).then_inc(ready, 1)
                    nc.gpsimd.iota(iota_row[:], [[1, 512]], base=0, channel_multiplier=0, allow_small_or_imprecise_dtypes=True)
                    nc.gpsimd.iota(pair_no[:], [[P, PC]], base=0, channel_multiplier=1, allow_small_or_imprecise_dtypes=True)
            project(nc, x, w, kv_dram, Qs, ident, ready)
            plan(nc, src, dst, srcp, dstp, tq_dram, TAB, IDX, trow, ident, ones, iota_row, pair_no)
            edges(nc, kv_dram, Qs, acc, mx, TAB, IDX, trow, ident, iota_row)
        nodes(nc, x, w, out, acc, ident)


_W = ["Wq", "bq", "Wk", "bk", "Wv", "bv", "Wskip", "bskip", "Wo", "bo", "W1", "b1", "W2", "b2", "g1", "be1", "g2", "be2"]


def kernel(**inputs):
    import numpy as _np
    import concourse.bacc as _bacc
    from concourse import mybir as _mybir
    from concourse.bass_utils import run_bass_kernel_spmd as _run

    nc = _bacc.Bacc("TRN2", target_bir_lowering=False, num_devices=1)
    arrays, aps = {}, {}
    for name in ["x", "src", "dst"] + ["L0_gnn_" + n for n in _W]:
        a = _np.ascontiguousarray(inputs[name])
        arrays["in_" + name] = a
        aps[name] = nc.dram_tensor("in_" + name, a.shape, _mybir.dt.from_np(a.dtype), kind="ExternalInput").ap()
    out = nc.dram_tensor("out", (N, D), F32, kind="ExternalOutput").ap()
    gnn_program(nc, aps["x"], aps["src"], aps["dst"], {n: aps["L0_gnn_" + n] for n in _W}, out)
    r = _run(nc, [arrays], core_ids=[0])
    return r.results[0]["out"]
```

```python
import numpy as np
import concourse.bass as bass
from concourse import mybir
from concourse.alu_op_type import AluOpType as ALU
from contextlib import ExitStack

F32 = mybir.dt.float32
BF16 = mybir.dt.bfloat16
I16 = mybir.dt.int16
I32 = mybir.dt.int32
ACT = mybir.ActivationFunctionType
AX = mybir.AxisListType
DVE = mybir.EngineType.DVE
PE = mybir.EngineType.PE

P = 128
N, D, E = 6250, 256, 200000
H, HD, FF = 8, 32, 1024
HC = HD + 1
KC = D // P
FC = FF // P
NT = -(-N // P)
TAIL = N - (NT - 1) * P
J = 4
GE = J * P
NG = -(-E // GE)
EP = NG * GE
NQ = NG + NT - 1
PC = -(-NQ // P)
NP = PC * P
PAD_DST = 1 << 20
BIG = 1e30
SCALE = float(1.0 / np.sqrt(HD))
NTAB = 3 * J


def at(start, count, size):
    return bass.ds(start * size, count * size)


def wait(eng, sem, n):
    if isinstance(n, int) and n <= 0:
        return
    eng.wait_ge(sem, n)


def top(ap):
    wide = ap.bitcast(BF16)
    return wide[tuple([slice(None)] * (len(wide.shape) - 1) + [slice(1, None, 2)])]


def hold(eng, sem, n, passed):
    if isinstance(n, int) and n <= 0:
        return
    eng.wait_ge(sem, n)
    eng.sem_inc(passed, 1)


def row_bcast(vec, n):
    return bass.AP(vec.tensor, 0, [[0, P], [1, n]])


def project(nc, x, w, kv_dram, Qs, ident, ident_ready):
    with ExitStack() as ctx:
        sb = lambda n, s, d=F32: ctx.enter_context(nc.sbuf_tensor(n, s, d))
        sem = lambda n: ctx.enter_context(nc.semaphore(n))
        wkv = sb("wkv", [P, KC, 2 * D])
        wq = sb("wq", [P, KC, D])
        bkv = sb("bkv", [P, 2 * D])
        bq = sb("bq", [P, D])
        xin = sb("xin", [P, 4, D])
        xT = sb("xT", [P, 2, KC, P])
        kvo = sb("kvo", [P, 4, 2 * D])
        psX = ctx.enter_context(nc.psum_tensor("psX", [P, 2, 512], F32))
        psKV = ctx.enter_context(nc.psum_tensor("psKV", [P, 2, 512], F32))
        psQp = ctx.enter_context(nc.psum_tensor("psQp", [P, 2, 512], F32))
        w_in = sem("w_in")
        b_in = sem("b_in")
        x_in = [sem(f"x_in{s}") for s in range(4)]
        xt_ps = sem("xt_ps")
        xt_sb = sem("xt_sb")
        proj_ps = sem("proj_ps")
        q_done = sem("q_done")
        kv_sb = sem("kv_sb")
        kv_out = [sem(f"kv_out{s}") for s in range(4)]

        def tiles(eng, step):
            for t in range(4):
                step(t, t, 0)
            with eng.Fori(4, NT - 4, 4) as i:
                for s in range(4):
                    step(i + s, s, i)
            step(NT - 1, (NT - 1) % 4, NT - 1)

        with nc.Block() as block:
            @block.sync
            def _(sp):
                def load(t, s, n4):
                    wait(sp, xt_ps, t - 3)
                    last = isinstance(t, int) and t == NT - 1
                    rows = TAIL if last else P
                    sp.dma_start(xin[0:rows, s, :], x[bass.ds(t * P, rows), :]).then_inc(x_in[s], 16)
                tiles(sp, load)

            @block.tensor
            def _(pe):
                pe.wait_ge(ident_ready, 2)
                pe.wait_ge(w_in, 3 * 16)
                def step(t, s, n4):
                    n = (n4 // 4) * 16 + 16 if isinstance(n4, int) else n4 * 4 + 16
                    pe.wait_ge(x_in[s], n)
                    wait(pe, xt_sb, t - 1)
                    for c in range(KC):
                        last = nc.tensor.transpose(psX[:, s % 2, c * P:(c + 1) * P], xin[:, s, c * P:(c + 1) * P], ident[:])
                    last.then_inc(xt_ps, 1)
                    pe.wait_ge(xt_sb, t + 1)
                    wait(pe, q_done, t - 1)
                    for c in range(KC):
                        nc.tensor.matmul(psKV[:, s % 2, :], xT[:, s % 2, c, :], wkv[:, c, :], start=c == 0, stop=c == KC - 1)
                    for c in range(KC):
                        last = nc.tensor.matmul(psQp[:, s % 2, 0:D], xT[:, s % 2, c, :], wq[:, c, :], start=c == 0, stop=c == KC - 1)
                    last.then_inc(proj_ps, 1)
                tiles(pe, step)

            @block.scalar
            def _(act):
                act.dma_start(wkv[:, :, 0:D], w["Wk"].rearrange("(c p) n -> p c n", p=P)).then_inc(w_in, 16)
                act.dma_start(wkv[:, :, D:2 * D], w["Wv"].rearrange("(c p) n -> p c n", p=P)).then_inc(w_in, 16)
                act.dma_start(wq[:], w["Wq"].rearrange("(c p) n -> p c n", p=P)).then_inc(w_in, 16)
                act.dma_start(bkv[:, 0:D], row_bcast(w["bk"], D)).then_inc(b_in, 16)
                act.dma_start(bkv[:, D:2 * D], row_bcast(w["bv"], D)).then_inc(b_in, 16)
                act.dma_start(bq[:], row_bcast(w["bq"], D)).then_inc(b_in, 16)

                def store(t, s, n4):
                    rows = TAIL if isinstance(t, int) and t == NT - 1 else P
                    act.wait_ge(kv_sb, t + 1)
                    act.dma_start(kv_dram[bass.ds(t * P, rows), :], kvo[0:rows, s, :]).then_inc(kv_out[s], 16)

                def step(t, s, n4):
                    act.wait_ge(xt_ps, t + 1)
                    wait(act, proj_ps, t - 1)
                    nc.scalar.copy(xT[:, s % 2].rearrange("p c n -> p (c n)"), psX[:, s % 2, 0:KC * P]).then_inc(xt_sb, 1)
                    if isinstance(t, int) and t == 0:
                        return
                    store(t - 1, (s - 1) % 4, n4)
                tiles(act, step)
                store(NT - 1, (NT - 1) % 4, 0)
                for s in range(4):
                    act.wait_ge(kv_out[s], 16 * len(range(s, NT, 4)))

            @block.vector
            def _(dve):
                dve.wait_ge(b_in, 3 * 16)

                def step(t, s, n4):
                    dve.wait_ge(proj_ps, t + 1)
                    if isinstance(n4, int):
                        if n4:
                            dve.wait_ge(kv_out[s], (n4 // 4) * 16)
                    else:
                        dve.wait_ge(kv_out[s], n4 * 4)
                    nc.vector.tensor_tensor(kvo[:, s, :], psKV[:, s % 2, :], bkv[:], ALU.add).then_inc(kv_sb, 1)
                    nc.vector.tensor_tensor(Qs[:, bass.ds(t, 1), :].rearrange("p a n -> p (a n)"), psQp[:, s % 2, 0:D], bq[:],
                                            ALU.add).then_inc(q_done, 1)
                tiles(dve, step)


def plan(nc, src, dst, srcp, dstp, tq_dram, TAB, IDX, trow, ident, pair_no):
    with ExitStack() as ctx:
        sb = lambda n, s, d=F32: ctx.enter_context(nc.sbuf_tensor(n, s, d))
        sem = lambda n: ctx.enter_context(nc.semaphore(n))
        padi = sb("padi", [1, 2, GE], I32)
        ones = sb("ones", [1, P])
        fl = sb("fl", [1, 2, NG], I32)
        flb = sb("flb", [1, 2, NG], I32)
        flf = sb("flf", [1, 2, NG])
        zrow = sb("zrow", [1, NG])
        cnt = sb("cnt", [1, NG])
        incl = sb("incl", [1, NG])
        start = sb("start", [1, 2, NG])
        cmpb = sb("cmpb", [P, NG])
        group_no = sb("group_no", [P, NG])
        grp = sb("grp", [P, PC])
        shift = sb("shift", [P, PC])
        blk = sb("blk", [P, PC])
        blk128 = sb("blk128", [P, PC])
        grpi = sb("grpi", [P, PC], I32)
        blki = sb("blki", [P, PC], I32)
        rows = sb("rows", [P, 2, PC, GE], I32)
        dstf = sb("dstf", [P, GE])
        edge = sb("edge", [P, 4, GE])
        psB = ctx.enter_context(nc.psum_tensor("psB", [P, 2, 512], F32))
        psT = ctx.enter_context(nc.psum_tensor("psT", [P, 4, 512], F32))
        padded = sem("padded")
        numbered = sem("numbered")
        pad_set = sem("pad_set")
        fl_in = sem("fl_in")
        v = sem("v")
        bc_ps = sem("bc_ps")
        rows_in = sem("rows_in")
        grp_ready = sem("grp_ready")
        tq_out = sem("tq_out")
        tq_in = sem("tq_in")
        edge_ready = sem("edge_ready")
        tr_ps = sem("tr_ps")
        tr_sb = sem("tr_sb")

        with nc.Block() as block:
            @block.sync
            def _(sp):
                sp.dma_start(srcp[0:E].rearrange("(a b) -> a b", a=16), src.rearrange("(a b) -> a b", a=16)).then_inc(padded, 16)
                sp.dma_start(dstp[0:E].rearrange("(a b) -> a b", a=16), dst.rearrange("(a b) -> a b", a=16)).then_inc(padded, 16)
                sp.wait_ge(pad_set, 2)
                sp.dma_start(srcp[E:EP][None, :], padi[0:1, 0, 0:EP - E]).then_inc(padded, 16)
                sp.dma_start(dstp[E:EP][None, :], padi[0:1, 1, 0:EP - E]).then_inc(padded, 16)
                with nc.allow_non_contiguous_dma("one element a group"):
                    sp.dma_start(fl[0:1, 0, :], bass.AP(dst.tensor, 0, [[0, 1], [GE, NG]])).then_inc(fl_in, 16)
                    sp.dma_start(fl[0:1, 1, 0:NG - 1], bass.AP(dst.tensor, GE - 1, [[0, 1], [GE, NG - 1]])).then_inc(fl_in, 16)
                    sp.dma_start(fl[0:1, 1, NG - 1:NG], bass.AP(dst.tensor, E - 1, [[0, 1], [1, 1]])).then_inc(fl_in, 16)
                    sp.wait_ge(grp_ready, 2)
                    sp.dma_start(tq_dram.rearrange("(c p) -> p c", p=P), blki[:]).then_inc(tq_out, 16)
                sp.wait_ge(tq_out, 16)
                sp.dma_start(trow[0:1, :], tq_dram[None, 0:NQ + 8]).then_inc(tq_in, 16)
                sp.wait_ge(tq_in, 16)

            @block.vector
            def _(dve):
                k = [0]

                def link(ins):
                    k[0] += 1
                    ins.then_inc(v, 1)
                    dve.wait_ge(v, k[0])
                nc.vector.memset(padi[:, 0, :], 0).then_inc(pad_set, 1)
                nc.vector.memset(padi[:, 1, :], PAD_DST).then_inc(pad_set, 1)
                nc.vector.memset(zrow[:], 0.0)
                dve.wait_ge(fl_in, 3 * 16)
                link(nc.vector.tensor_scalar(flb[:], fl[:], 7, None, ALU.arith_shift_right))
                link(nc.vector.tensor_copy(flf[:], flb[:]))
                link(nc.vector.tensor_tensor(cnt[:], flf[:, 1, :], flf[:, 0, :], ALU.subtract))
                link(nc.vector.tensor_scalar(cnt[:], cnt[:], 1.0, None, ALU.add))
                link(nc.vector.tensor_tensor_scan(incl[:], zrow[:], cnt[:], 0.0, ALU.add, ALU.add))
                link(nc.vector.tensor_tensor(start[:, 0, :], incl[:], cnt[:], ALU.subtract))
                nc.vector.tensor_tensor(start[:, 1, :], flf[:, 0, :], start[:, 0, :], ALU.subtract).then_inc(edge_ready, 1)
                dve.wait_ge(bc_ps, 1)
                dve.wait_ge(numbered, 2)
                for c in range(PC):
                    link(nc.vector.tensor_scalar(cmpb[:], psB[:, 0, 0:NG], pair_no[:, c:c + 1], None, ALU.is_le))
                    link(nc.vector.tensor_reduce(grp[:, c:c + 1], cmpb[:], AX.X, ALU.add))
                link(nc.vector.tensor_scalar(grp[:], grp[:], -1.0, None, ALU.add))
                nc.vector.tensor_copy(grpi[:], grp[:]).then_inc(grp_ready, 1)
                for c in range(PC):
                    link(nc.vector.tensor_scalar(cmpb[:], group_no[:], grp[:, c:c + 1], None, ALU.is_equal))
                    link(nc.vector.tensor_tensor(cmpb[:], psB[:, 1, 0:NG], cmpb[:], ALU.mult))
                    link(nc.vector.tensor_reduce(shift[:, c:c + 1], cmpb[:], AX.X, ALU.add))
                link(nc.vector.tensor_tensor(blk[:], shift[:], pair_no[:], ALU.add))
                link(nc.vector.tensor_scalar(blk128[:], blk[:], float(P), None, ALU.mult))
                link(nc.vector.tensor_scalar(blk[:], blk[:], float(NT - 1), None, ALU.min))
                nc.vector.tensor_copy(blki[:], blk[:]).then_inc(grp_ready, 1)
                for c in range(PC):
                    dve.wait_ge(rows_in, 32 * (c + 1))
                    link(nc.vector.tensor_copy(dstf[:], rows[:, 1, c, :]))
                    nc.vector.tensor_copy(edge[:, 3, :], rows[:, 0, c, :])
                    nc.vector.tensor_scalar(edge[:, 0, :], dstf[:], blk128[:, c:c + 1], None, ALU.subtract)
                    link(nc.vector.tensor_tensor(edge[:, 1, 0:GE - 1], dstf[:, 1:GE], dstf[:, 0:GE - 1], ALU.not_equal))
                    link(nc.vector.tensor_scalar(edge[:, 2, 1:GE], edge[:, 1, 0:GE - 1], -BIG, None, ALU.mult))
                    link(nc.vector.memset(edge[:, 1, P - 1:GE:P], 1.0))
                    nc.vector.memset(edge[:, 2, 0:GE:P], -BIG).then_inc(edge_ready, 1)
                    for a in range(4):
                        dve.wait_ge(tr_ps, c * 4 + a + 1)
                        to = min((c + 1) * P, NQ)
                        got = psT[:, a, :].rearrange("p (j g) -> p g j", j=J)[:, 0:to - c * P, :]
                        if a < 3:
                            out = TAB[:, c * P:to, a * J:(a + 1) * J]
                        else:
                            out = IDX[:, c * P:to, :]
                        nc.vector.tensor_copy(out, got).then_inc(tr_sb, 1)

            @block.gpsimd
            def _(pool):
                nc.gpsimd.memset(ones[:], 1.0).then_inc(numbered, 1)
                nc.gpsimd.iota(group_no[:], [[1, NG]], base=0, channel_multiplier=0, allow_small_or_imprecise_dtypes=True).then_inc(numbered, 1)
                pool.wait_ge(padded, 4 * 16)
                pool.wait_ge(grp_ready, 1)
                for c in range(PC):
                    for k, lst in ((0, srcp), (1, dstp)):
                        if c or k:
                            pool.wait_ge(rows_in, 16 * (2 * c + k))
                        nc.gpsimd.indirect_dma_start(
                            rows[:, k, c, :], None, lst.rearrange("(a b) -> a b", b=GE),
                            bass.IndirectOffsetOnAxis(ap=grpi[:, c:c + 1], axis=0)).then_inc(rows_in, 16)

            @block.tensor
            def _(pe):
                pe.wait_ge(edge_ready, 1)
                pe.wait_ge(numbered, 2)
                for k in range(2):
                    last = nc.tensor.matmul(psB[:, k, 0:NG], ones[:], start[:, k, :], start=True, stop=True)
                last.then_inc(bc_ps, 1)
                for c in range(PC):
                    pe.wait_ge(edge_ready, 2 + c)
                    for a in range(4):
                        n = c * 4 + a
                        if n >= 4:
                            pe.wait_ge(tr_sb, n - 3)
                        for j in range(J):
                            last = nc.tensor.transpose(psT[:, a, j * P:(j + 1) * P], edge[:, a, j * P:(j + 1) * P], ident[:])
                        last.then_inc(tr_ps, 1)


def edges(nc, kv_dram, Qs, acc, mx, TAB, IDX, trow, ident, iota_row):
    with ExitStack() as ctx:
        sb = lambda n, s, d=F32: ctx.enter_context(nc.sbuf_tensor(n, s, d))
        ps = lambda n, s: ctx.enter_context(nc.psum_tensor(n, s, F32))
        sem = lambda n: ctx.enter_context(nc.semaphore(n))
        R = 6
        kv = sb("kv", [P, R, J, 2 * D])
        cols = sb("cols", [P, R, 2 * J])
        brkb = sb("brkb", [P, R, J, H])
        idx = sb("idx", [P, R, J], I32)
        oh = sb("oh", [P, R, J, P])
        ohT = sb("ohT", [P, R, J, P])
        prod = sb("prod", [P, J * D])
        lg = sb("lg", [P, 3, J * H])
        msk = sb("msk", [J * H, 2, P])
        run = sb("run", [J * H, 2, P])
        last9 = sb("last9", [P, R, J, H + 1])
        absent = sb("absent", [P, J])
        cand = sb("cand", [P, J, H])
        qmax = sb("qmax", [P, H])
        rest9 = sb("rest9", [P, 2, 2, J, H + 1])
        mnew = sb("mnew", [P, 2, 3, H])
        md = sb("md", [P, R, H])
        arg = sb("arg", [P, 2, J * H])
        cf = sb("cf", [P, R, H])
        msg = sb("msg", [P, 2, J, H, HC])
        psQ = ps("psQ", [P, J * D])
        psHT = ps("psHT", [P, 512])
        psO = ps("psO", [P, 2, 512])
        psL = ps("psL", [P, 512])
        psM = ps("psM", [P, 512])
        psS = ps("psS", [P, 512])
        sLT = psL[0:J * H, 0:P]
        sMK = psM[0:J * H, 0:P]
        sME = psL[:, P:P + J * H]
        sST = psS[:, 0:J * H]
        sNM = psS[:, J * H:J * H + J * (H + 1)]

        names = ("cols_ready idx_ready sq_ready oh_ready oht_ps oht_sb q_half prod_half l_ready mask_ps mask_sb lt_ps scan_done st_ps sl_ready "
                 "nmax_ps sl_whole sl_rest m_rest md_ready msg_last absent_ok cand_ok qmax_ok mnew_ok m_ready m_kept mexp_ps arg_ready p_ready c_ready msg_ready seg_ps acc_scaled acc_done passed").split()
        S = {n: sem(n) for n in names}
        kv_in = [sem(f"kv_in{s}") for s in range(R)]
        init = sem("init")
        FIRST, LEAD, LAG = 7, 4, 4
        TURNS = (NQ - LEAD - FIRST) // R

        def steps(eng, step, reads=None):
            engine = eng.engine
            for i in range(-LEAD, FIRST):
                step(i, i, read_blocks(engine, i, reads), 0, None, None)
            if reads:
                k0, n = reads
                regs = [eng.alloc_register(f"blocks{k}") for k in range(n)]
                eng.load(regs, trow[0:1, FIRST + k0:FIRST + k0 + n])
            with eng.Fori(0, TURNS) as turn:
                i = eng.snap(turn * R + FIRST)
                ts = {k0 + k: eng.snap(r, min_val=0, max_val=NT - 1) for k, r in enumerate(regs)} if reads else {}
                for s in range(R):
                    ahead = (lambda: eng.load(regs, trow[0:1, bass.ds(i + (R + k0), n)])) if reads and s == R - 2 else None
                    step(i + s, FIRST + s, ts, s, turn, ahead)
            for i in range(FIRST + R * TURNS, NQ + LAG):
                step(i, i, read_blocks(engine, i, reads), 0, None, None)

        def has(i, k):
            return not isinstance(i, int) or 0 <= i + k < NQ

        def read_blocks(engine, i, reads):
            ks = [k for k in range(reads[0], reads[0] + reads[1] - R + 1) if 0 <= i + k < NQ] if reads else []
            if not ks:
                return {}
            _, ts = nc.values_load_multi_w_load_instructions(trow[0:1, i + ks[0]:i + ks[-1] + 1], engines=[engine], min_val=0, max_val=NT - 1)
            return dict(zip(ks, ts))

        with nc.Block() as block:
            @block.gpsimd
            def _(pool):
                pool.wait_ge(init, 1)

                def gather(q, s, js):
                    for j in js:
                        nc.gpsimd.indirect_dma_start(
                            kv[:, s % R, j, :], None, kv_dram[:, :],
                            bass.IndirectOffsetOnAxis(ap=idx[:, s % R, j:j + 1], axis=0)).then_inc(kv_in[s % R], 16)

                def step(i, s, ts, off, turn, ahead):
                    if has(i, -4):
                        ac = acc[:, bass.ds(ts[off - 4], 1)].rearrange("p a h c -> p (a h) c")
                        pool.wait_ge(S["c_ready"], i - 3)
                        wait(pool, S["acc_done"], i - 4)
                        nc.gpsimd.tensor_tensor(ac, ac, cf[:, (s - 4) % R, :].rearrange("p (h a) -> p h a", a=1).to_broadcast([P, H, HC]), ALU.mult).then_inc(S["acc_scaled"], 1)
                    if has(i, 2):
                        hold(pool, S["idx_ready"], i + 3, S["passed"])
                        hold(pool, S["msg_ready"], i + 3 - R, S["passed"])
                        hold(pool, S["msg_last"], i + 3 - R, S["passed"])
                        gather(i + 2, s + 2, (0, 1))
                    if has(i, -3):
                        pool.wait_ge(S["p_ready"], i - 2)
                        nc.gpsimd.tensor_tensor(msg[:, (s - 3) % 2, J - 1, :, 0:HD], kv[:, (s - 3) % R, J - 1, D:2 * D].rearrange("p (h c) -> p h c", h=H),
                                                msg[:, (s - 3) % 2, J - 1, :, HD:HC].to_broadcast([P, H, HD]), ALU.mult).then_inc(S["msg_last"], 1)
                    if has(i, 2):
                        gather(i + 2, s + 2, (2, 3))
                    if ahead:
                        ahead()
                steps(pool, step, (-4, R))

            @block.scalar
            def _(act):
                def columns(q, s):
                    s = s % R
                    ent = TAB[:, bass.ds(q, 1), :]
                    nc.scalar.copy(idx[:, s, :], IDX[:, bass.ds(q, 1), :].rearrange("p a n -> p (a n)")).then_inc(S["idx_ready"], 1)
                    nc.scalar.copy(cols[:, s, :], ent[:, :, 0:2 * J].rearrange("p a n -> p (a n)"))
                    nc.scalar.copy(last9[:, s, :, H:H + 1], ent[:, :, J:2 * J].rearrange("p a n -> p n a"))
                    nc.scalar.copy(brkb[:, s], ent[:, :, 2 * J:3 * J].rearrange("p a n -> p n a").to_broadcast([P, J, H])).then_inc(S["cols_ready"], 1)

                def onehot(q, s):
                    s = s % R
                    act.wait_ge(S["cols_ready"], q + 1)
                    wait(act, S["seg_ps"], q - R + 1)
                    for j in range(J):
                        last = nc.scalar.activation(oh[:, s, j, :], iota_row[:], ACT.Square, bias=cols[:, s, j:j + 1], scale=-1.0)
                    last.then_inc(S["sq_ready"], 1)
                    act.wait_ge(S["sq_ready"], q + 1)
                    nc.scalar.activation(oh[:, s], oh[:, s], ACT.Relu, bias=1.0, scale=-1.0).then_inc(S["oh_ready"], 1)

                def step(i, s, ts, off, turn, ahead):
                    if has(i, 1):
                        act.wait_ge(S["oht_ps"], i + 2)
                        wait(act, S["mexp_ps"], i + 2 - R)
                        nc.scalar.copy(ohT[:, (s + 1) % R], psHT[:].rearrange("p (j n) -> p j n", j=J)).then_inc(S["oht_sb"], 1)
                    if has(i, 0):
                        act.wait_ge(S["mask_ps"], i + 1)
                        wait(act, S["scan_done"], i - 1)
                        nc.scalar.copy(msk[:, s % 2, :], sMK).then_inc(S["mask_sb"], 1)
                    if has(i, -2):
                        act.wait_ge(S["md_ready"], i - 1)
                        nc.scalar.activation(cf[:, (s - 2) % R, :], md[:, (s - 2) % R, :], ACT.Exp, scale=SCALE).then_inc(S["c_ready"], 1)
                    if has(i, 4):
                        wait(act, S["nmax_ps"], i - 1)
                        columns(i + 4, s + 4)
                    if has(i, 2):
                        onehot(i + 2, s + 2)
                    if has(i, -2):
                        act.wait_ge(S["arg_ready"], i - 1)
                        wait(act, S["seg_ps"], i - 3)
                        nc.scalar.activation(msg[:, s % 2, :, :, HD:HC], arg[:, s % 2, :].rearrange("p (j h a) -> p j h a", j=J, a=1),
                                             ACT.Exp, scale=SCALE).then_inc(S["p_ready"], 1)
                act.wait_ge(init, 1)
                steps(act, step)

            @block.tensor
            def _(pe):
                def expand_q(q, s, t, half):
                    if half == 0:
                        pe.wait_ge(S["oht_sb"], q + 1)
                    wait(pe, S["prod_half"], 2 * q - 1 + half)
                    for j in (2 * half, 2 * half + 1):
                        last = nc.tensor.matmul(psQ[:, j * D:(j + 1) * D], ohT[:, s % R, j, :],
                                                Qs[:, bass.ds(t, 1), :].rearrange("p a n -> p (a n)"), start=True, stop=True)
                    last.then_inc(S["q_half"], 1)

                def step(i, s, ts, off, turn, ahead):
                    t = ts.get(off + 1)
                    if has(i, -1):
                        pe.wait_ge(S["l_ready"], 2 * i)
                        wait(pe, S["arg_ready"], i - 2)
                        nc.tensor.transpose(sLT, lg[:, (s - 1) % 3, :], ident[:]).then_inc(S["lt_ps"], 1)
                    if has(i, 0):
                        pe.wait_ge(S["cols_ready"], i + 1)
                        wait(pe, S["mask_sb"], i)
                        nc.tensor.transpose(sMK, brkb[:, s % R].rearrange("p j h -> p (j h)"), ident[:]).then_inc(S["mask_ps"], 1)
                    if has(i, 1):
                        pe.wait_ge(S["oh_ready"], i + 2)
                        wait(pe, S["oht_sb"], i + 1)
                        for j in range(J):
                            last = nc.tensor.transpose(psHT[:, j * P:(j + 1) * P], oh[:, (s + 1) % R, j, :], ident[:])
                        last.then_inc(S["oht_ps"], 1)
                    if has(i, -4):
                        pe.wait_ge(S["msg_ready"], i - 3)
                        pe.wait_ge(S["msg_last"], i - 3)
                        wait(pe, S["acc_done"], i - 5)
                        for j in range(J):
                            last = nc.tensor.matmul(psO[:, s % 2, 0:H * HC], oh[:, (s - 4) % R, j, :], msg[:, s % 2, j].rearrange("p h c -> p (h c)"),
                                                    start=j == 0, stop=j == J - 1)
                        last.then_inc(S["seg_ps"], 1)
                    if ahead:
                        ahead()
                    if has(i, -1):
                        hold(pe, S["scan_done"], i, S["passed"])
                        hold(pe, S["cand_ok"], i - 1, S["passed"])
                        nc.tensor.transpose(sST, run[:, (s - 1) % 2, :], ident[0:J * H, 0:J * H]).then_inc(S["st_ps"], 1)
                    if has(i, 1):
                        expand_q(i + 1, s + 1, t, 0)
                    if has(i, -2):
                        pe.wait_ge(S["m_ready"], i - 1)
                        for j in range(J):
                            for k in range(3):
                                last = nc.tensor.matmul(sME[:, j * H:(j + 1) * H], top(ohT[:, (s - 2) % R, j, :]), top(mnew[:, s % 2, k, :]), start=k == 0, stop=k == 2)
                        last.then_inc(S["mexp_ps"], 1)
                    if has(i, -1):
                        pe.wait_ge(S["sl_ready"], i)
                        for j in range(J):
                            for k, part in enumerate((last9[:, (s - 1) % R, j, :], rest9[:, (s - 1) % 2, 0, j, :], rest9[:, (s - 1) % 2, 1, j, :])):
                                last = nc.tensor.matmul(sNM[:, j * (H + 1):(j + 1) * (H + 1)], top(oh[:, (s - 1) % R, j, :]), top(part), start=k == 0, stop=k == 2)
                        last.then_inc(S["nmax_ps"], 1)
                    if has(i, 1):
                        expand_q(i + 1, s + 1, t, 1)
                steps(pe, step, (1, R))

            @block.vector
            def _(dve):
                def logits_half(i, s, half):
                    dve.wait_ge(S["q_half"], i * 2 + 1 + half)
                    if half == 0:
                        dve.wait_ge(kv_in[s[0] % R], (s[0] // R + 1) * J * 16 if s[1] is None else s[1] * (J * 16) + (s[0] // R + 1) * J * 16)
                    wait(dve, S["l_ready"], 2 * i - 1 + half)
                    cs, js = slice(2 * half * D, (2 * half + 2) * D), slice(2 * half, 2 * half + 2)
                    nc.vector.tensor_tensor(prod[:, cs].rearrange("p (j n) -> p j n", j=2), psQ[:, cs].rearrange("p (j n) -> p j n", j=2),
                                            kv[:, s[0] % R, js, 0:D], ALU.mult).then_inc(S["prod_half"], 1)

                def sum_half(i, s, half):
                    dve.wait_ge(S["prod_half"], i * 2 + 1 + half)
                    cs, gs = slice(2 * half * D, (2 * half + 2) * D), slice(2 * half * H, (2 * half + 2) * H)
                    nc.vector.tensor_reduce(lg[:, s % 3, gs], prod[:, cs].rearrange("p (g c) -> p g c", c=HD), AX.X, ALU.add).then_inc(S["l_ready"], 1)

                def bc(ap, n):
                    return ap.rearrange("p (a o) -> p a o", o=1).to_broadcast([P, ap.shape[1], n])

                def step(i, s, ts, off, turn, ahead):
                    now, runs, maxima, msgs, sums = has(i, 0), has(i, -1), has(i, -2), has(i, -3), has(i, -4)
                    s1, s2 = s - 1, s - 2
                    if maxima:
                        mcur = mx[:, bass.ds(ts[off - 2], 1), :].rearrange("p a h -> p (a h)")
                        m = mnew[:, s2 % 2]
                        nm = sNM.rearrange("p (j h) -> p j h", j=J)
                    if now:
                        logits_half(i, (s, turn), 0)
                    if maxima:
                        dve.wait_ge(S["nmax_ps"], i - 1)
                        nc.vector.tensor_scalar(absent[:].rearrange("p (j a) -> p j a", a=1), nm[:, :, H:H + 1], BIG, -BIG, ALU.mult, ALU.add).then_inc(S["absent_ok"], 1)
                    if runs:
                        dve.wait_ge(S["lt_ps"], i)
                        dve.wait_ge(S["mask_sb"], i)
                        nc.vector.tensor_tensor_scan(run[:, s1 % 2, :], msk[:, s1 % 2, :], sLT, -BIG, ALU.add, ALU.max).then_inc(S["scan_done"], 1)
                    if maxima:
                        dve.wait_ge(S["absent_ok"], i - 1)
                        nc.vector.tensor_tensor(cand[:], nm[:, :, 0:H], bc(absent[:], H), ALU.add).then_inc(S["cand_ok"], 1)
                    if now:
                        logits_half(i, (s, turn), 1)
                    if maxima:
                        dve.wait_ge(S["cand_ok"], i - 1)
                        nc.vector.tensor_reduce(qmax[:], cand[:].rearrange("p j h -> p h j"), AX.X, ALU.max).then_inc(S["qmax_ok"], 1)
                    if now:
                        sum_half(i, s, 0)
                    if maxima:
                        dve.wait_ge(S["qmax_ok"], i - 1)
                        wait(dve, S["m_kept"], i - 2)
                        nc.vector.tensor_tensor(m[:, 0, :], mcur, qmax[:], ALU.max).then_inc(S["mnew_ok"], 1)
                    if now:
                        sum_half(i, s, 1)
                    if ahead:
                        ahead()
                    if maxima:
                        dve.wait_ge(S["mnew_ok"], i - 1)
                        nc.vector.tensor_tensor(m[:, 1, :], m[:, 0, :], top(m[:, 0, :]), ALU.subtract).then_inc(S["m_rest"], 1)
                        nc.vector.tensor_tensor(md[:, s2 % R, :], mcur, m[:, 0, :], ALU.subtract).then_inc(S["md_ready"], 1)
                    if runs:
                        dve.wait_ge(S["st_ps"], i)
                        nc.vector.tensor_tensor(last9[:, s1 % R, :, 0:H], sST.rearrange("p (j h) -> p j h", j=J), bc(cols[:, s1 % R, J:2 * J], H), ALU.mult).then_inc(S["sl_whole"], 1)
                    if maxima:
                        dve.wait_ge(S["m_rest"], i - 1)
                        nc.vector.tensor_tensor(m[:, 2, :], m[:, 1, :], top(m[:, 1, :]), ALU.subtract).then_inc(S["m_ready"], 1)
                        dve.wait_ge(S["md_ready"], i - 1)
                        nc.vector.tensor_tensor(mcur, m[:, 0, :], m[:, 0, :], ALU.max).then_inc(S["m_kept"], 1)
                    if runs:
                        dve.wait_ge(S["sl_whole"], i)
                        nc.vector.tensor_tensor(rest9[:, s1 % 2, 0], last9[:, s1 % R], top(last9[:, s1 % R]), ALU.subtract).then_inc(S["sl_rest"], 1)
                    if sums:
                        ac = acc[:, bass.ds(ts[off - 4], 1)].rearrange("p a h c -> p (a h) c")
                        dve.wait_ge(S["acc_scaled"], i - 3)
                        dve.wait_ge(S["seg_ps"], i - 3)
                        nc.vector.tensor_tensor(ac, ac, psO[:, s % 2, 0:H * HC].rearrange("p (h c) -> p h c", h=H), ALU.add).then_inc(S["acc_done"], 1)
                    if runs:
                        dve.wait_ge(S["sl_rest"], i)
                        nc.vector.tensor_tensor(rest9[:, s1 % 2, 1], rest9[:, s1 % 2, 0], top(rest9[:, s1 % 2, 0]), ALU.subtract).then_inc(S["sl_ready"], 1)
                    if msgs:
                        dve.wait_ge(S["p_ready"], i - 2)
                        nc.vector.tensor_tensor(msg[:, (s - 3) % 2, 0:J - 1, :, 0:HD], kv[:, (s - 3) % R, 0:J - 1, D:2 * D].rearrange("p j (h c) -> p j h c", h=H),
                                                msg[:, (s - 3) % 2, 0:J - 1, :, HD:HC].to_broadcast([P, J - 1, H, HD]), ALU.mult).then_inc(S["msg_ready"], 1)
                    if maxima:
                        dve.wait_ge(S["mexp_ps"], i - 1)
                        nc.vector.tensor_tensor(arg[:, s % 2, :], lg[:, s2 % 3, :], sME, ALU.subtract).then_inc(S["arg_ready"], 1)

                nc.vector.memset(acc[:].rearrange("p a h c -> p (a h c)"), 0.0)
                nc.vector.memset(mx[:], -BIG).then_inc(init, 1)
                dve.wait_ge(init, 1)
                steps(dve, step, (-4, R + 2))
                dve.wait_ge(S["acc_done"], NQ)


def nodes(nc, x, w, out, acc, ident):
    with ExitStack() as ctx:
        sb = lambda n, s, d=F32: ctx.enter_context(nc.sbuf_tensor(n, s, d))
        ps = lambda n, s: ctx.enter_context(nc.psum_tensor(n, s, F32))
        sem = lambda n: ctx.enter_context(nc.semaphore(n))
        R, FIRST, LAG = 6, 7, 5
        TURNS = (NT - FIRST) // R
        assert (NT - FIRST) % R == 0
        wsk = sb("wsk", [P, KC, D])
        wo = sb("wo", [P, KC, D])
        w1 = sb("w1", [P, KC, FF])
        w2 = sb("w2", [P, FC, D])
        rows = {n: sb(f"r_{n}", [P, D]) for n in ("bskip", "bo", "b2", "g1", "be1", "g2", "be2")}
        b1c = sb("b1c", [P, FC])
        xin = sb("nx", [P, R, D])
        xT = sb("nxT", [P, KC * P])
        saT = sb("saT", [P, KC * P])
        x1T = sb("x1T", [P, KC * P])
        den = sb("den", [P, H])
        att = sb("att", [P, D])
        sa = sb("sa", [P, 2, D])
        xb = sb("xb", [P, 2, D])
        y = sb("y", [P, D])
        y2 = sb("y2", [P, D])
        x1 = sb("x1", [P, 2, D])
        x1b = sb("x1b", [P, R, D])
        hT = sb("hT", [P, 2, FC, P])
        z = sb("z", [P, D])
        zz = sb("zz", [P, 2, D])
        st = sb("st", [P, 3, 6])
        ag = sb("ag", [P, 3, 2])
        sd = sb("sd", [P, 3, 1])
        rs = sb("rs", [P, 3, 1])
        ob = sb("ob", [P, 2, D])
        eps = sb("eps", [P, 1])
        pX = ps("pX", [P, 512])
        pA = ps("pA", [P, 512])
        pC = ps("pC", [P, 512])
        pS = ps("pS", [P, 512])
        pB = ps("pB", [P, 512])
        pH = ps("pH", [P, 2, 512])
        pF = ps("pF", [P, 512])
        w_in = sem("nw_in")
        x_in = [sem(f"nx_in{s}") for s in range(R)]
        out_done = [sem(f"out_done{s}") for s in range(2)]
        names = ("xt_ps xt_sb skip_ps sa_ready sat_ps sat_sb wo_ps x1_ready x1t_ps x1t_sb h_ps h_sb f_ps xb_ready x1b_ready n1_ready n2_ready zz_ready "
                 "y_read z_read o_ready p1 pv den1 den2 att1 att2 bn0 bn1 bn2 rs0 rs1 rs2 eps_ok passed stat0 stat1 stat2 root0 root1 root2").split()
        S = {n: sem("n_" + n) for n in names}

        def steps(eng, step):
            for i in range(0, FIRST):
                step(i, i, None)
            with eng.Fori(0, TURNS) as turn:
                i = eng.snap(turn * R + FIRST)
                for s in range(R):
                    step(i + s, FIRST + s, turn)
            for i in range(NT, NT + LAG):
                step(i, i, None)

        def has(i, k):
            return not isinstance(i, int) or 0 <= i + k < NT

        with nc.Block() as block:
            @block.sync
            def _(sp):
                for t, d in ((wsk, "Wskip"), (wo, "Wo"), (w1, "W1")):
                    sp.dma_start(t[:], w[d].rearrange("(c p) n -> p c n", p=P)).then_inc(w_in, 16)
                sp.dma_start(w2[:], w["W2"].rearrange("(c p) n -> p c n", p=P)).then_inc(w_in, 16)
                for n, t in rows.items():
                    sp.dma_start(t[:], row_bcast(w[n], D)).then_inc(w_in, 16)
                with nc.allow_non_contiguous_dma("a bias by partitions"):
                    sp.dma_start(b1c[:], w["b1"].rearrange("(c p) -> p c", p=P)).then_inc(w_in, 16)

                def load(t, s, r=P):
                    wait(sp, S["zz_ready"], t - R + 1)
                    sp.dma_start(xin[0:r, s % R, :], x[bass.ds(t * P, r), :]).then_inc(x_in[s % R], 16)
                for t in range(R):
                    load(t, t)
                with sp.Fori(R, NT - R, R) as i:
                    for s in range(R):
                        load(i + s, s)
                load(NT - 1, NT - 1, TAIL)
                assert NT % R == 1

            @block.tensor
            def _(pe):
                pe.wait_ge(w_in, 12 * 16)

                def turn_over(dst, src_, done):
                    for c in range(KC):
                        last = nc.tensor.transpose(dst[:, c * P:(c + 1) * P], src_[:, c * P:(c + 1) * P], ident[:])
                    last.then_inc(done, 1)

                def step(i, s, turn):
                    if has(i, 0):
                        pe.wait_ge(x_in[s % R], (s // R + 1) * 16 if turn is None else turn * 16 + (s // R + 1) * 16)
                        turn_over(pX, xin[:, s % R, :], S["xt_ps"])
                    if has(i, -1):
                        pe.wait_ge(S["sa_ready"], i)
                        turn_over(pA, sa[:, (s - 1) % 2, :], S["sat_ps"])
                    if has(i, -2):
                        pe.wait_ge(S["x1_ready"], i - 1)
                        turn_over(pC, x1[:, s % 2, :], S["x1t_ps"])
                    if has(i, 0):
                        pe.wait_ge(S["xt_sb"], i + 1)
                        wait(pe, S["sa_ready"], i)
                        for c in range(KC):
                            last = nc.tensor.matmul(pS[:, 0:D], xT[:, c * P:(c + 1) * P], wsk[:, c, :], start=c == 0, stop=c == KC - 1)
                        last.then_inc(S["skip_ps"], 1)
                    if has(i, -1):
                        pe.wait_ge(S["sat_sb"], i)
                        wait(pe, S["y_read"], i - 1)
                        for c in range(KC):
                            last = nc.tensor.matmul(pB[:, 0:D], saT[:, c * P:(c + 1) * P], wo[:, c, :], start=c == 0, stop=c == KC - 1)
                        last.then_inc(S["wo_ps"], 1)
                    if has(i, -2):
                        pe.wait_ge(S["x1t_sb"], i - 1)
                        for f in range(FC):
                            if f % 4 == 0:
                                wait(pe, S["h_sb"], (i - 3) * 2 + f // 4 + 1 if has(i, -3) else 0)
                            for c in range(KC):
                                last = nc.tensor.matmul(pH[:, f // 4, (f % 4) * P:(f % 4 + 1) * P], w1[:, c, f * P:(f + 1) * P], x1T[:, c * P:(c + 1) * P],
                                                        start=c == 0, stop=c == KC - 1)
                            if f % 4 == 3:
                                last.then_inc(S["h_ps"], 1)
                    if has(i, -3):
                        pe.wait_ge(S["h_sb"], (i - 3) * 2 + 2)
                        wait(pe, S["z_read"], i - 3)
                        for f in range(FC):
                            last = nc.tensor.matmul(pF[:, 0:D], hT[:, (s - 3) % 2, f, :], w2[:, f, :], start=f == 0, stop=f == FC - 1)
                        last.then_inc(S["f_ps"], 1)
                steps(pe, step)

            @block.scalar
            def _(act):
                act.wait_ge(S["eps_ok"], 1)
                act.wait_ge(w_in, 12 * 16)

                def root(k, t):
                    act.wait_ge(S[f"stat{k}"], t + 1)
                    nc.scalar.activation(sd[:, k, :], ag[:, k, 1:2], ACT.Sqrt, bias=eps[:]).then_inc(S[f"root{k}"], 1)

                def relu(i, s, bank):
                    act.wait_ge(S["h_ps"], (i - 2) * 2 + bank + 1)
                    if bank == 0:
                        wait(act, S["f_ps"], i - 3)
                    for f in range(4 * bank, 4 * bank + 4):
                        last = nc.scalar.activation(hT[:, s % 2, f, :], pH[:, bank, (f % 4) * P:(f % 4 + 1) * P], ACT.Relu, bias=b1c[:, f:f + 1])
                    last.then_inc(S["h_sb"], 1)

                def step(i, s, turn):
                    if has(i, 0):
                        act.wait_ge(S["xt_ps"], i + 1)
                        wait(act, S["skip_ps"], i)
                        nc.scalar.copy(xT[:], pX[:, 0:KC * P]).then_inc(S["xt_sb"], 1)
                    if has(i, -1):
                        act.wait_ge(S["sat_ps"], i)
                        wait(act, S["wo_ps"], i - 1)
                        nc.scalar.copy(saT[:], pA[:, 0:KC * P]).then_inc(S["sat_sb"], 1)
                    if has(i, -2):
                        act.wait_ge(S["x1t_ps"], i - 1)
                        wait(act, S["h_ps"], (i - 3) * 2 + 2 if has(i, -3) else 0)
                        nc.scalar.copy(x1T[:], pC[:, 0:KC * P]).then_inc(S["x1t_sb"], 1)
                    if has(i, -5):
                        root(2, i - 5)
                    if has(i, -4):
                        root(1, i - 4)
                    if has(i, -2):
                        relu(i, s, 0)
                    if has(i, -1):
                        root(0, i - 1)
                    if has(i, -2):
                        relu(i, s, 1)
                steps(act, step)

            @block.gpsimd
            def _(pool):
                def step(i, s, turn):
                    if has(i, 0):
                        pool.wait_ge(x_in[s % R], (s // R + 1) * 16 if turn is None else turn * 16 + (s // R + 1) * 16)
                        wait(pool, S["y_read"], i - 1)
                        nc.gpsimd.tensor_tensor(xb[:, s % 2, :], xin[:, s % R, :], rows["bo"][:], ALU.add).then_inc(S["xb_ready"], 1)
                    if has(i, -4):
                        t = i - 4
                        pool.wait_ge(S["n2_ready"], t + 1)
                        nc.gpsimd.tensor_tensor(z[:], z[:], rows["g2"][:], ALU.mult).then_inc(S["pv"], 1)
                        pool.wait_ge(S["pv"], (i - 4) * 2 + 1)
                        nc.gpsimd.tensor_tensor(z[:], z[:], rows["be2"][:], ALU.add).then_inc(S["pv"], 1)
                        pool.wait_ge(S["pv"], (i - 4) * 2 + 2)
                        wait(pool, S["o_ready"], t - 1)
                        nc.gpsimd.tensor_tensor(zz[:, s % 2, :], z[:], xin[:, (s - 4) % R, :], ALU.add).then_inc(S["zz_ready"], 1)
                    if has(i, -1):
                        t = i - 1
                        pool.wait_ge(S["n1_ready"], i)
                        nc.gpsimd.tensor_tensor(y2[:], y2[:], rows["g1"][:], ALU.mult).then_inc(S["p1"], 1)
                        pool.wait_ge(S["p1"], i)
                        wait(pool, S["x1t_ps"], i - 2)
                        nc.gpsimd.tensor_tensor(x1[:, (s - 1) % 2, :], y2[:], rows["be1"][:], ALU.add).then_inc(S["x1_ready"], 1)
                        pool.wait_ge(S["x1_ready"], i)
                        wait(pool, S["z_read"], i - R)
                        nc.gpsimd.tensor_tensor(x1b[:, (s - 1) % R, :], x1[:, (s - 1) % 2, :], rows["b2"][:], ALU.add).then_inc(S["x1b_ready"], 1)
                    if has(i, -5):
                        store(i - 5, s - 5, P)

                def store(t, s, r):
                    pool.wait_ge(S["o_ready"], t + 1)
                    if isinstance(t, int) and t == NT - 1:
                        r = TAIL
                    pool.dma_start(out[bass.ds(t * P, r), :], ob[0:r, s % 2, :]).then_inc(out_done[s % 2], 16)
                pool.wait_ge(w_in, 12 * 16)
                steps(pool, step)
                pool.wait_ge(out_done[0], 16 * len(range(0, NT, 2)))
                pool.wait_ge(out_done[1], 16 * len(range(1, NT, 2)))

            @block.vector
            def _(dve):
                nc.vector.memset(eps[:], 1e-5).then_inc(S["eps_ok"], 1)
                dve.wait_ge(w_in, 12 * 16)

                def stats(k, t, in_):
                    nc.vector.bn_stats(st[:, k, :], in_).then_inc(S[f"bn{k}"], 1)
                    hold(dve, S[f"bn{k}"], t + 1, S["passed"])
                    nc.vector.bn_aggr(ag[:, k, :], st[:, k, :]).then_inc(S[f"stat{k}"], 1)

                def normed(k, t, out_, in_):
                    dve.wait_ge(S[f"root{k}"], t + 1)
                    nc.vector.reciprocal(rs[:, k, :], sd[:, k, :]).then_inc(S[f"rs{k}"], 1)
                    dve.wait_ge(S[f"rs{k}"], t + 1)
                    return nc.vector.tensor_scalar(out_, in_, ag[:, k, 0:1], rs[:, k, 0:1], ALU.subtract, ALU.mult)

                def step(i, s, turn):
                    if has(i, -5):
                        t = i - 5
                        dve.wait_ge(S["zz_ready"], t + 1)
                        stats(2, t, zz[:, (s - 5) % 2, :])
                    if has(i, -4):
                        t = i - 4
                        dve.wait_ge(S["f_ps"], t + 1)
                        dve.wait_ge(S["x1b_ready"], t + 1)
                        wait(dve, S["zz_ready"], t)
                        nc.vector.tensor_tensor(z[:], x1b[:, (s - 4) % R, :], pF[:, 0:D], ALU.add).then_inc(S["z_read"], 1)
                        dve.wait_ge(S["z_read"], t + 1)
                        stats(1, t, z[:])
                    if has(i, -5):
                        t = i - 5
                        if turn is None:
                            wait(dve, out_done[(s - 5) % 2], (t // 2) * 16)
                        else:
                            dve.wait_ge(out_done[(s - 5) % 2], turn * (R // 2 * 16) + ((s - 5) // 2) * 16)
                        n = normed(2, t, ob[:, (s - 5) % 2, :], zz[:, (s - 5) % 2, :])
                        n.then_inc(S["o_ready"], 1)
                    if has(i, 0):
                        ac = acc[:, bass.ds(i, 1)].rearrange("p a h c -> p (a h) c")
                        nc.vector.tensor_scalar(den[:].rearrange("p (h a) -> p h a", a=1), ac[:, :, HD:HC], 1e-16, None, ALU.add).then_inc(S["den1"], 1)
                        dve.wait_ge(S["den1"], i + 1)
                        nc.vector.reciprocal(den[:], den[:]).then_inc(S["den2"], 1)
                    if has(i, -4):
                        normed(1, i - 4, z[:], z[:]).then_inc(S["n2_ready"], 1)
                    if has(i, 0):
                        dve.wait_ge(S["den2"], i + 1)
                        nc.vector.tensor_tensor(att[:].rearrange("p (h c) -> p h c", h=H), ac[:, :, 0:HD],
                                                den[:].rearrange("p (h a) -> p h a", a=1).to_broadcast([P, H, HD]), ALU.mult).then_inc(S["att1"], 1)
                        dve.wait_ge(S["att1"], i + 1)
                        nc.vector.tensor_tensor(att[:], att[:], rows["bskip"][:], ALU.add).then_inc(S["att2"], 1)
                        dve.wait_ge(S["att2"], i + 1)
                        dve.wait_ge(S["skip_ps"], i + 1)
                        wait(dve, S["sat_ps"], i - 1)
                        nc.vector.tensor_tensor(sa[:, s % 2, :], att[:], pS[:, 0:D], ALU.add).then_inc(S["sa_ready"], 1)
                    if has(i, -1):
                        t = i - 1
                        dve.wait_ge(S["wo_ps"], i)
                        dve.wait_ge(S["xb_ready"], i)
                        nc.vector.tensor_tensor(y[:], xb[:, (s - 1) % 2, :], pB[:, 0:D], ALU.add).then_inc(S["y_read"], 1)
                        dve.wait_ge(S["y_read"], i)
                        stats(0, t, y[:])
                        wait(dve, S["x1_ready"], i - 1)
                        normed(0, t, y2[:], y[:]).then_inc(S["n1_ready"], 1)
                steps(dve, step)


def gnn_program(nc, x, src, dst, w, out):
    kv_dram = nc.dram_tensor("kv_table", (N, 2 * D), F32, kind="Internal").ap()
    srcp = nc.dram_tensor("src_padded", (EP,), I32, kind="Internal").ap()
    dstp = nc.dram_tensor("dst_padded", (EP,), I32, kind="Internal").ap()
    tq_dram = nc.dram_tensor("pair_block", (NP,), I32, kind="Internal").ap()
    with ExitStack() as ctx:
        sb = lambda n, s, d=F32: ctx.enter_context(nc.sbuf_tensor(n, s, d))
        ident = sb("ident", [P, P])
        iota_row = sb("iota_row", [P, P])
        pair_no = sb("pair_no", [P, PC])
        acc = sb("acc", [P, NT, H, HC])
        ready = ctx.enter_context(nc.semaphore("const_ready"))
        with ExitStack() as c2:
            sb2 = lambda n, s, d=F32: c2.enter_context(nc.sbuf_tensor(n, s, d))
            Qs = sb2("Qs", [P, NT, D])
            mx = sb2("mx", [P, NT, H])
            TAB = sb2("TAB", [P, NQ, NTAB], BF16)
            IDX = sb2("IDX", [P, NQ, J], I16)
            trow = sb2("trow", [1, NQ + 8], I32)
            with nc.Block() as block:
                @block.gpsimd
                def _(pool):
                    nc.gpsimd.memset(ident[:], 0.0).then_inc(ready, 1)
                    pool.wait_ge(ready, 1)
                    nc.gpsimd.affine_select(ident[:], ident[:], [[-1, P]], ALU.not_equal, 1.0, base=0, channel_multiplier=1).then_inc(ready, 1)
                    nc.gpsimd.iota(iota_row[:], [[1, P]], base=0, channel_multiplier=0, allow_small_or_imprecise_dtypes=True)
                    nc.gpsimd.iota(pair_no[:], [[P, PC]], base=0, channel_multiplier=1, allow_small_or_imprecise_dtypes=True)
            project(nc, x, w, kv_dram, Qs, ident, ready)
            plan(nc, src, dst, srcp, dstp, tq_dram, TAB, IDX, trow, ident, pair_no)
            edges(nc, kv_dram, Qs, acc, mx, TAB, IDX, trow, ident, iota_row)
        nodes(nc, x, w, out, acc, ident)


_W = ["Wq", "bq", "Wk", "bk", "Wv", "bv", "Wskip", "bskip", "Wo", "bo", "W1", "b1", "W2", "b2", "g1", "be1", "g2", "be2"]


def kernel(**inputs):
    import numpy as _np
    import concourse.bacc as _bacc
    from concourse import mybir as _mybir
    from concourse.bass_utils import run_bass_kernel_spmd as _run

    nc = _bacc.Bacc("TRN2", target_bir_lowering=False, num_devices=1)
    arrays, aps = {}, {}
    for name in ["x", "src", "dst"] + ["L0_gnn_" + n for n in _W]:
        a = _np.ascontiguousarray(inputs[name])
        arrays["in_" + name] = a
        aps[name] = nc.dram_tensor("in_" + name, a.shape, _mybir.dt.from_np(a.dtype), kind="ExternalInput").ap()
    out = nc.dram_tensor("out", (N, D), F32, kind="ExternalOutput").ap()
    gnn_program(nc, aps["x"], aps["src"], aps["dst"], {n: aps["L0_gnn_" + n] for n in _W}, out)
    r = _run(nc, [arrays], core_ids=[0])
    return r.results[0]["out"]
```

```python
import numpy as np
import concourse.bass as bass
from concourse import mybir
from concourse.alu_op_type import AluOpType as ALU
from contextlib import ExitStack

F32 = mybir.dt.float32
BF16 = mybir.dt.bfloat16
I16 = mybir.dt.int16
I32 = mybir.dt.int32
ACT = mybir.ActivationFunctionType
AX = mybir.AxisListType

P = 128
N, D, E = 6250, 256, 200000
H, HD, FF = 8, 32, 1024
HC = HD + 1
KC = D // P
FC = FF // P
NT = -(-N // P)
TAIL = N - (NT - 1) * P
J = 4
GE = J * P
NG = -(-E // GE)
EP = NG * GE
NQ = NG + NT - 1
TE = 125
NTE = E // TE
assert E % TE == 0
PC = -(-NQ // P)
NP = PC * P
PAD_DST = 1 << 20
BIG = 1e30
SCALE = float(1.0 / np.sqrt(HD))
NTAB = 3 * J


def wait(eng, sem, n):
    if isinstance(n, int) and n <= 0:
        return
    eng.wait_ge(sem, n)


def top(ap):
    wide = ap.bitcast(BF16)
    return wide[tuple([slice(None)] * (len(wide.shape) - 1) + [slice(1, None, 2)])]


def hold(eng, sem, n, passed):
    if isinstance(n, int) and n <= 0:
        return
    eng.wait_ge(sem, n)
    eng.sem_inc(passed, 1)


def row_bcast(vec, n):
    return bass.AP(vec.tensor, 0, [[0, P], [1, n]])


def project(nc, x, w, kv_dram, Qs, ident, ident_ready, src, dst, srcp, dstp, descents_dram, disorder, acc, mx):
    with ExitStack() as ctx:
        sb = lambda n, s, d=F32: ctx.enter_context(nc.sbuf_tensor(n, s, d))
        sem = lambda n: ctx.enter_context(nc.semaphore(n))
        wkv = sb("wkv", [P, KC, 2 * D])
        wq = sb("wq", [P, KC, D])
        bkv = sb("bkv", [P, 2 * D])
        bq = sb("bq", [P, D])
        xin = sb("xin", [P, 4, D])
        xT = sb("xT", [P, 2, KC, P])
        kvo = sb("kvo", [P, 4, 2 * D])
        padi = sb("padi", [1, 2, EP - E], I32)
        dsti = sb("dsti", [TE, NTE + 1], I32)
        desc = sb("desc", [TE, NTE])
        descents = sb("descents", [TE, 1])
        descent_row = sb("descent_row", [1, TE])
        descent = sb("descent", [1, 1])
        psX = ctx.enter_context(nc.psum_tensor("psX", [P, 2, 512], F32))
        psKV = ctx.enter_context(nc.psum_tensor("psKV", [P, 2, 512], F32))
        psQp = ctx.enter_context(nc.psum_tensor("psQp", [P, 2, 512], F32))
        w_in = sem("w_in")
        b_in = sem("b_in")
        pad_set = sem("pad_set")
        padded = sem("padded")
        dsti_in = sem("dsti_in")
        compared = sem("compared")
        descents_ok = sem("descents_ok")
        descents_out = sem("descents_out")
        descents_in = sem("descents_in")
        x_in = [sem(f"x_in{s}") for s in range(4)]
        xt_ps = sem("xt_ps")
        xt_sb = sem("xt_sb")
        proj_ps = sem("proj_ps")
        q_done = sem("q_done")
        kv_sb = sem("kv_sb")
        kv_out = [sem(f"kv_out{s}") for s in range(4)]

        def tiles(eng, step):
            for t in range(4):
                step(t, t, 0)
            with eng.Fori(4, NT - 4, 4) as i:
                for s in range(4):
                    step(i + s, s, i)
            step(NT - 1, (NT - 1) % 4, NT - 1)

        with nc.Block() as block:
            @block.sync
            def _(sp):
                def load(t, s, n4):
                    wait(sp, xt_ps, t - 3)
                    last = isinstance(t, int) and t == NT - 1
                    rows = TAIL if last else P
                    sp.dma_start(xin[0:rows, s, :], x[bass.ds(t * P, rows), :]).then_inc(x_in[s], 16)
                tiles(sp, load)

            @block.tensor
            def _(pe):
                pe.wait_ge(ident_ready, 2)
                pe.wait_ge(w_in, 3 * 16)
                def turn_over(t, s, n):
                    pe.wait_ge(x_in[s], n * 16)
                    wait(pe, xt_sb, t - 1)
                    for c in range(KC):
                        last = nc.tensor.transpose(psX[:, s % 2, c * P:(c + 1) * P], xin[:, s, c * P:(c + 1) * P], ident[:])
                    last.then_inc(xt_ps, 1)
                turn_over(0, 0, 1)

                def step(t, s, n4):
                    n = n4 // 4
                    if not isinstance(t, int) or t < NT - 1:
                        turn_over(t + 1, (s + 1) % 4, n + (1 if s < 3 else 2))
                    pe.wait_ge(xt_sb, t + 1)
                    wait(pe, q_done, t - 1)
                    for c in range(KC):
                        nc.tensor.matmul(psKV[:, s % 2, :], xT[:, s % 2, c, :], wkv[:, c, :], start=c == 0, stop=c == KC - 1)
                    for c in range(KC):
                        last = nc.tensor.matmul(psQp[:, s % 2, 0:D], xT[:, s % 2, c, :], wq[:, c, :], start=c == 0, stop=c == KC - 1)
                    last.then_inc(proj_ps, 1)
                tiles(pe, step)

            @block.scalar
            def _(act):
                act.dma_start(wkv[:, :, 0:D], w["Wk"].rearrange("(c p) n -> p c n", p=P)).then_inc(w_in, 16)
                act.dma_start(wkv[:, :, D:2 * D], w["Wv"].rearrange("(c p) n -> p c n", p=P)).then_inc(w_in, 16)
                act.dma_start(wq[:], w["Wq"].rearrange("(c p) n -> p c n", p=P)).then_inc(w_in, 16)
                act.dma_start(bkv[:, 0:D], row_bcast(w["bk"], D)).then_inc(b_in, 16)
                act.dma_start(bkv[:, D:2 * D], row_bcast(w["bv"], D)).then_inc(b_in, 16)
                act.dma_start(bq[:], row_bcast(w["bq"], D)).then_inc(b_in, 16)

                def store(t, s, n4):
                    rows = TAIL if isinstance(t, int) and t == NT - 1 else P
                    act.wait_ge(kv_sb, t + 1)
                    act.dma_start(kv_dram[bass.ds(t * P, rows), :], kvo[0:rows, s, :]).then_inc(kv_out[s], 16)

                def step(t, s, n4):
                    act.wait_ge(xt_ps, t + 1)
                    wait(act, proj_ps, t - 1)
                    nc.scalar.copy(xT[:, s % 2].rearrange("p c n -> p (c n)"), psX[:, s % 2, 0:KC * P]).then_inc(xt_sb, 1)
                    if isinstance(t, int) and t == 0:
                        return
                    store(t - 1, (s - 1) % 4, n4)
                tiles(act, step)
                store(NT - 1, (NT - 1) % 4, 0)
                for s in range(4):
                    act.wait_ge(kv_out[s], 16 * len(range(s, NT, 4)))

            @block.gpsimd
            def _(pool):
                pool.wait_ge(pad_set, 1)
                pool.dma_start(dsti[0:TE - 1, :], bass.AP(dst.tensor, 0, [[NTE, TE - 1], [1, NTE + 1]])).then_inc(dsti_in, 16)
                pool.dma_start(dsti[TE - 1:TE, 0:NTE], dst[E - NTE:E][None, :]).then_inc(dsti_in, 16)
                pool.wait_ge(w_in, 3 * 16)
                pool.dma_start(srcp[0:E].rearrange("(a b) -> a b", a=16), src.rearrange("(a b) -> a b", a=16)).then_inc(padded, 16)
                pool.dma_start(dstp[0:E].rearrange("(a b) -> a b", a=16), dst.rearrange("(a b) -> a b", a=16)).then_inc(padded, 16)
                pool.wait_ge(pad_set, 3)
                pool.dma_start(srcp[E:EP][None, :], padi[0:1, 0, :]).then_inc(padded, 16)
                pool.dma_start(dstp[E:EP][None, :], padi[0:1, 1, :]).then_inc(padded, 16)
                pool.wait_ge(descents_ok, 1)
                pool.dma_start(descents_dram[:, None], descents[:]).then_inc(descents_out, 16)
                pool.wait_ge(descents_out, 16)
                pool.dma_start(descent_row[:], descents_dram[None, :]).then_inc(descents_in, 16)
                nc.gpsimd.memset(mx[:], -BIG)
                nc.gpsimd.memset(acc[:].rearrange("p a h c -> p (a h c)"), 0.0)
                pool.wait_ge(padded, 4 * 16)

            @block.vector
            def _(dve):
                nc.vector.memset(dsti[:, NTE:NTE + 1], PAD_DST).then_inc(pad_set, 1)
                nc.vector.memset(padi[:, 0, :], 0).then_inc(pad_set, 1)
                nc.vector.memset(padi[:, 1, :], PAD_DST).then_inc(pad_set, 1)
                dve.wait_ge(dsti_in, 2 * 16)
                nc.vector.tensor_tensor(desc[:], dsti[:, 0:NTE], dsti[:, 1:NTE + 1], ALU.is_gt).then_inc(compared, 1)
                dve.wait_ge(compared, 1)
                nc.vector.tensor_reduce(descents[:], desc[:], AX.X, ALU.max).then_inc(descents_ok, 1)
                dve.wait_ge(b_in, 3 * 16)

                def step(t, s, n4):
                    dve.wait_ge(proj_ps, t + 1)
                    if isinstance(n4, int):
                        if n4:
                            dve.wait_ge(kv_out[s], (n4 // 4) * 16)
                    else:
                        dve.wait_ge(kv_out[s], n4 * 4)
                    nc.vector.tensor_tensor(kvo[:, s, :], psKV[:, s % 2, :], bkv[:], ALU.add).then_inc(kv_sb, 1)
                    nc.vector.tensor_tensor(Qs[:, bass.ds(t, 1), :].rearrange("p a n -> p (a n)"), psQp[:, s % 2, 0:D], bq[:],
                                            ALU.add).then_inc(q_done, 1)
                tiles(dve, step)
                dve.wait_ge(descents_in, 16)
                nc.vector.tensor_reduce(descent[:], descent_row[:], AX.X, ALU.max).then_inc(compared, 1)
                dve.wait_ge(compared, 2)
                nc.vector.tensor_copy(disorder[:], descent[:])


def sort_edges(nc, src, dst, srcp, dstp, counter_dram, iota_row, pair_no, disorder):
    with ExitStack() as ctx:
        sb = lambda n, s, d=F32: ctx.enter_context(nc.sbuf_tensor(n, s, d))
        sem = lambda n: ctx.enter_context(nc.semaphore(n))
        zeros = sb("zeros", [P, NT], I32)
        earlier = sb("earlier", [TE, TE])
        drow = sb("drow", [TE, TE], I32)
        dcol = sb("dcol", [TE, 1], I32)
        scol = sb("scol", [TE, 1], I32)
        drowf = sb("drowf", [TE, TE])
        dcolf = sb("dcolf", [TE, 1])
        same = sb("same", [TE, TE])
        before = sb("before", [TE, TE])
        n_same = sb("n_same", [TE, 1])
        n_before = sb("n_before", [TE, 1])
        got = sb("got", [TE, 1], I32)
        gotf = sb("gotf", [TE, 1])
        nextf = sb("nextf", [TE, 1])
        placef = sb("placef", [TE, 1])
        next_ = sb("next_", [TE, 1], I32)
        place = sb("place", [TE, 1], I32)
        counts = sb("counts", [1, N], I32)
        countf = sb("countf", [1, N])
        ends = sb("ends", [1, N])
        zeros_ok = sem("zeros_ok")
        counter_set = sem("counter_set")
        counts_in = sem("counts_in")
        starts_ok = sem("starts_ok")
        row_in = [sem(f"row_in{k}") for k in range(2)]
        col_in = [sem(f"col_in{k}") for k in range(2)]
        scol_in = [sem(f"scol_in{k}") for k in range(2)]
        got_in = [sem(f"got_in{k}") for k in range(2)]
        link = [sem(f"link{k}") for k in range(2)]
        next_ok = [sem(f"next_ok{k}") for k in range(2)]
        next_out = [sem(f"next_out{k}") for k in range(2)]
        src_out = sem("src_out")
        dst_out = sem("dst_out")
        prefix = sem("prefix")
        passed = sem("sort_passed")
        counters = counter_dram[:, None]

        with nc.Block() as block:
            @block.gpsimd
            def _(pool):
                def at_node():
                    return bass.IndirectOffsetOnAxis(ap=dcol[:], axis=0)

                with pool.If(pool.value_load(disorder[0:1, 0:1], min_val=0, max_val=1) > 0):
                    pool.wait_ge(zeros_ok, 1)
                    pool.dma_start(counter_dram.rearrange("(p a) -> p a", p=P), zeros[:]).then_inc(counter_set, 16)
                    pool.wait_ge(counter_set, 16)
                    for k in range(2):
                        if k == 1:
                            pool.dma_start(counts[:], counter_dram[None, 0:N]).then_inc(counts_in, 16)
                            pool.wait_ge(starts_ok, 1)
                            pool.dma_start(counter_dram[None, 0:N], counts[:]).then_inc(counter_set, 16)
                            pool.wait_ge(counter_set, 32)
                        with pool.Fori(0, NTE) as t:
                            tile = bass.ds(t * TE, TE)
                            pool.dma_start(dcol[:], dst[tile][:, None]).then_inc(col_in[k], 16)
                            pool.dma_start(scol[:], src[tile][:, None]).then_inc(scol_in[k], 16)
                            pool.dma_start(drow[:], dst[tile].partition_broadcast(TE)).then_inc(row_in[k], 16)
                            hold(pool, col_in[k], t * 16 + 16, passed)
                            nc.gpsimd.indirect_dma_start(got[:], None, counters, at_node()).then_inc(got_in[k], 16)
                            hold(pool, next_ok[k], t + 1, passed)
                            nc.gpsimd.indirect_dma_start(counters, at_node(), next_[:], None).then_inc(next_out[k], 16)
                            if k == 1:
                                hold(pool, scol_in[k], t * 16 + 16, passed)
                                nc.gpsimd.indirect_dma_start(srcp[:, None], bass.IndirectOffsetOnAxis(ap=place[:], axis=0), scol[:], None).then_inc(src_out, 16)
                                nc.gpsimd.indirect_dma_start(dstp[:, None], bass.IndirectOffsetOnAxis(ap=place[:], axis=0), dcol[:], None).then_inc(dst_out, 16)
                                pool.wait_ge(src_out, t * 16 + 16)
                                pool.wait_ge(dst_out, t * 16 + 16)
                            pool.wait_ge(scol_in[k], t * 16 + 16)
                            pool.wait_ge(next_out[k], t * 16 + 16)

            @block.vector
            def _(dve):
                with dve.If(dve.value_load(disorder[0:1, 0:1], min_val=0, max_val=1) > 0):
                    nc.vector.memset(zeros[:], 0).then_inc(zeros_ok, 1)
                    nc.vector.tensor_scalar(earlier[:], iota_row[0:TE, 0:TE], pair_no[0:TE, 0:1], None, ALU.is_lt)
                    for k in range(2):
                        if k == 1:
                            dve.wait_ge(counts_in, 16)
                            nc.vector.tensor_copy(countf[:], counts[:]).then_inc(prefix, 1)
                            dve.wait_ge(prefix, 1)
                            nc.vector.tensor_tensor_scan(ends[:], countf[:], countf[:], 0.0, ALU.add, ALU.max).then_inc(prefix, 1)
                            dve.wait_ge(prefix, 2)
                            nc.vector.tensor_tensor(ends[:], ends[:], countf[:], ALU.subtract).then_inc(prefix, 1)
                            dve.wait_ge(prefix, 3)
                            nc.vector.tensor_copy(counts[:], ends[:]).then_inc(starts_ok, 1)
                        with dve.Fori(0, NTE) as t:
                            dve.wait_ge(row_in[k], t * 16 + 16)
                            dve.wait_ge(col_in[k], t * 16 + 16)
                            nc.vector.tensor_copy(drowf[:], drow[:])
                            nc.vector.tensor_copy(dcolf[:], dcol[:]).then_inc(link[k], 1)
                            dve.wait_ge(link[k], t * 5 + 1)
                            nc.vector.tensor_scalar(same[:], drowf[:], dcolf[:, 0:1], None, ALU.is_equal).then_inc(link[k], 1)
                            dve.wait_ge(link[k], t * 5 + 2)
                            nc.vector.tensor_tensor(before[:], same[:], earlier[:], ALU.mult)
                            nc.vector.tensor_reduce(n_same[:], same[:], AX.X, ALU.add).then_inc(link[k], 1)
                            dve.wait_ge(link[k], t * 5 + 3)
                            nc.vector.tensor_reduce(n_before[:], before[:], AX.X, ALU.add)
                            dve.wait_ge(got_in[k], t * 16 + 16)
                            nc.vector.tensor_copy(gotf[:], got[:]).then_inc(link[k], 1)
                            dve.wait_ge(link[k], t * 5 + 4)
                            nc.vector.tensor_tensor(nextf[:], gotf[:], n_same[:], ALU.add)
                            nc.vector.tensor_tensor(placef[:], gotf[:], n_before[:], ALU.add).then_inc(link[k], 1)
                            dve.wait_ge(link[k], t * 5 + 5)
                            nc.vector.tensor_copy(place[:], placef[:])
                            nc.vector.tensor_copy(next_[:], nextf[:]).then_inc(next_ok[k], 1)


def plan(nc, srcp, dstp, tq_dram, TAB, IDX, trow, ident, pair_no):
    with ExitStack() as ctx:
        sb = lambda n, s, d=F32: ctx.enter_context(nc.sbuf_tensor(n, s, d))
        sem = lambda n: ctx.enter_context(nc.semaphore(n))
        ones = sb("ones", [1, P])
        fl = sb("fl", [1, 2, NG], I32)
        flb = sb("flb", [1, 2, NG], I32)
        flf = sb("flf", [1, 2, NG])
        zrow = sb("zrow", [1, NG])
        cnt = sb("cnt", [1, NG])
        incl = sb("incl", [1, NG])
        start = sb("start", [1, 2, NG])
        cmpb = sb("cmpb", [P, NG])
        group_no = sb("group_no", [P, NG])
        grp = sb("grp", [P, PC])
        shift = sb("shift", [P, PC])
        blk = sb("blk", [P, PC])
        blk128 = sb("blk128", [P, PC])
        grpi = sb("grpi", [P, PC], I32)
        blki = sb("blki", [P, PC], I32)
        rows = sb("rows", [P, 2, PC, GE], I32)
        dstf = sb("dstf", [P, GE])
        edge = sb("edge", [P, 2, 4, GE])
        psB = ctx.enter_context(nc.psum_tensor("psB", [P, 2, 512], F32))
        psT = ctx.enter_context(nc.psum_tensor("psT", [P, 4, 512], F32))
        numbered = sem("numbered")
        fl_in = sem("fl_in")
        chained = sem("chained")
        bc_ps = sem("bc_ps")
        rows_in = [sem(f"rows_in{c}") for c in range(PC)]
        grp_ready = sem("grp_ready")
        tq_out = sem("tq_out")
        tq_in = sem("tq_in")
        edge_ready = sem("edge_ready")
        tr_ps = sem("tr_ps")
        tr_sb = sem("tr_sb")

        with nc.Block() as block:
            @block.sync
            def _(sp):
                with nc.allow_non_contiguous_dma("one element a group"):
                    sp.dma_start(fl[0:1, 0, :], bass.AP(dstp.tensor, 0, [[0, 1], [GE, NG]])).then_inc(fl_in, 16)
                    sp.dma_start(fl[0:1, 1, 0:NG - 1], bass.AP(dstp.tensor, GE - 1, [[0, 1], [GE, NG - 1]])).then_inc(fl_in, 16)
                    sp.dma_start(fl[0:1, 1, NG - 1:NG], bass.AP(dstp.tensor, E - 1, [[0, 1], [1, 1]])).then_inc(fl_in, 16)
                    sp.wait_ge(grp_ready, 2)
                    sp.dma_start(tq_dram.rearrange("(c p) -> p c", p=P), blki[:]).then_inc(tq_out, 16)
                sp.wait_ge(tq_out, 16)
                sp.dma_start(trow[0:1, :], tq_dram[None, 0:NQ + 8]).then_inc(tq_in, 16)
                sp.wait_ge(tq_in, 16)

            @block.vector
            def _(dve):
                k = [0]

                def link(ins):
                    k[0] += 1
                    ins.then_inc(chained, 1)
                    dve.wait_ge(chained, k[0])
                nc.vector.memset(zrow[:], 0.0)
                dve.wait_ge(fl_in, 3 * 16)
                link(nc.vector.tensor_scalar(flb[:], fl[:], 7, None, ALU.arith_shift_right))
                link(nc.vector.tensor_copy(flf[:], flb[:]))
                link(nc.vector.tensor_tensor(cnt[:], flf[:, 1, :], flf[:, 0, :], ALU.subtract))
                link(nc.vector.tensor_scalar(cnt[:], cnt[:], 1.0, None, ALU.add))
                link(nc.vector.tensor_tensor_scan(incl[:], zrow[:], cnt[:], 0.0, ALU.add, ALU.add))
                link(nc.vector.tensor_tensor(start[:, 0, :], incl[:], cnt[:], ALU.subtract))
                nc.vector.tensor_tensor(start[:, 1, :], flf[:, 0, :], start[:, 0, :], ALU.subtract).then_inc(edge_ready, 1)
                dve.wait_ge(bc_ps, 1)
                dve.wait_ge(numbered, 2)
                for c in range(PC):
                    link(nc.vector.tensor_scalar(cmpb[:], psB[:, 0, 0:NG], pair_no[:, c:c + 1], None, ALU.is_le))
                    link(nc.vector.tensor_reduce(grp[:, c:c + 1], cmpb[:], AX.X, ALU.add))
                link(nc.vector.tensor_scalar(grp[:], grp[:], -1.0, None, ALU.add))
                nc.vector.tensor_copy(grpi[:], grp[:]).then_inc(grp_ready, 1)
                for c in range(PC):
                    link(nc.vector.tensor_scalar(cmpb[:], group_no[:], grp[:, c:c + 1], None, ALU.is_equal))
                    link(nc.vector.tensor_tensor(cmpb[:], psB[:, 1, 0:NG], cmpb[:], ALU.mult))
                    link(nc.vector.tensor_reduce(shift[:, c:c + 1], cmpb[:], AX.X, ALU.add))
                link(nc.vector.tensor_tensor(blk[:], shift[:], pair_no[:], ALU.add))
                link(nc.vector.tensor_scalar(blk128[:], blk[:], float(P), None, ALU.mult))
                link(nc.vector.tensor_scalar(blk[:], blk[:], float(NT - 1), None, ALU.min))
                nc.vector.tensor_copy(blki[:], blk[:]).then_inc(grp_ready, 1)
                for c in range(PC):
                    dve.wait_ge(rows_in[c], 2 * 16)
                    if c >= 2:
                        dve.wait_ge(tr_ps, (c - 1) * 4)
                    local, last, first, source = (edge[:, c % 2, a, :] for a in range(4))
                    link(nc.vector.tensor_copy(dstf[:], rows[:, 1, c, :]))
                    nc.vector.tensor_copy(source, rows[:, 0, c, :])
                    nc.vector.tensor_scalar(local, dstf[:], blk128[:, c:c + 1], None, ALU.subtract)
                    link(nc.vector.tensor_tensor(last[:, 0:GE - 1], dstf[:, 1:GE], dstf[:, 0:GE - 1], ALU.not_equal))
                    link(nc.vector.tensor_scalar(first[:, 1:GE], last[:, 0:GE - 1], -BIG, None, ALU.mult))
                    nc.vector.memset(last[:, P - 1:GE:P], 1.0)
                    nc.vector.memset(first[:, 0:GE:P], -BIG).then_inc(edge_ready, 1)

            @block.scalar
            def _(act):
                for c in range(PC):
                    for a in range(4):
                        act.wait_ge(tr_ps, c * 4 + a + 1)
                        to = min((c + 1) * P, NQ)
                        got = psT[:, a, :].rearrange("p (j g) -> p g j", j=J)[:, 0:to - c * P, :]
                        out = TAB[:, c * P:to, a * J:(a + 1) * J] if a < 3 else IDX[:, c * P:to, :]
                        nc.scalar.copy(out, got).then_inc(tr_sb, 1)

            @block.gpsimd
            def _(pool):
                nc.gpsimd.memset(ones[:], 1.0).then_inc(numbered, 1)
                nc.gpsimd.iota(group_no[:], [[1, NG]], base=0, channel_multiplier=0, allow_small_or_imprecise_dtypes=True).then_inc(numbered, 1)
                pool.wait_ge(grp_ready, 1)
                for c in range(PC):
                    for k, lst in ((0, srcp), (1, dstp)):
                        nc.gpsimd.indirect_dma_start(
                            rows[:, k, c, :], None, lst.rearrange("(a b) -> a b", b=GE),
                            bass.IndirectOffsetOnAxis(ap=grpi[:, c:c + 1], axis=0)).then_inc(rows_in[c], 16)

            @block.tensor
            def _(pe):
                pe.wait_ge(edge_ready, 1)
                pe.wait_ge(numbered, 2)
                for k in range(2):
                    last = nc.tensor.matmul(psB[:, k, 0:NG], ones[:], start[:, k, :], start=True, stop=True)
                last.then_inc(bc_ps, 1)
                for c in range(PC):
                    pe.wait_ge(edge_ready, 2 + c)
                    for a in range(4):
                        n = c * 4 + a
                        if n >= 4:
                            pe.wait_ge(tr_sb, n - 3)
                        for j in range(J):
                            last = nc.tensor.transpose(psT[:, a, j * P:(j + 1) * P], edge[:, c % 2, a, j * P:(j + 1) * P], ident[:])
                        last.then_inc(tr_ps, 1)


def edges(nc, kv_dram, Qs, acc, mx, TAB, IDX, trow, ident, iota_row):
    with ExitStack() as ctx:
        sb = lambda n, s, d=F32: ctx.enter_context(nc.sbuf_tensor(n, s, d))
        ps = lambda n, s: ctx.enter_context(nc.psum_tensor(n, s, F32))
        sem = lambda n: ctx.enter_context(nc.semaphore(n))
        R = 6
        kv = sb("kv", [P, R, J, 2 * D])
        cols = sb("cols", [P, R, 2 * J])
        brkb = sb("brkb", [P, R, J, H], BF16)
        idx = sb("idx", [P, R, J], I32)
        oh = sb("oh", [P, R, J, P])
        ohT = sb("ohT", [P, R, J, P])
        prod = sb("prod", [P, J * D])
        lg = sb("lg", [P, 3, J * H])
        msk = sb("msk", [J * H, 2, P])
        run = sb("run", [J * H, 2, P])
        last9 = sb("last9", [P, R, J, H + 1])
        absent = sb("absent", [P, J])
        cand = sb("cand", [P, J, H])
        qmax = sb("qmax", [P, H])
        rest9 = sb("rest9", [P, 2, 2, J, H + 1])
        mnew = sb("mnew", [P, 2, 3, H])
        md = sb("md", [P, 2, H])
        arg = sb("arg", [P, 2, J * H])
        cf = sb("cf", [P, R, H])
        msg = sb("msg", [P, 2, J, H, HC])
        psQ = ps("psQ", [P, J * D])
        psHT = ctx.enter_context(nc.psum_tensor("psHT", [P, J * P], BF16))
        psO = ps("psO", [P, 2, 512])
        psL = ps("psL", [P, 512])
        psM = ctx.enter_context(nc.psum_tensor("psM", [P, 1024], BF16))
        psS = ps("psS", [P, 512])
        sLT = psL[0:J * H, 0:P]
        sMK = psM[0:J * H, 0:P]
        sME = psL[:, P:P + J * H]
        sST = psS[:, 0:J * H]
        sNM = psS[:, J * H:J * H + J * (H + 1)]

        names = ("cols_ready idx_ready sq_ready oh_ready oht_ps oht_sb q_half prod_half l_ready mask_ps mask_sb lt_ps scan_done st_ps sl_ready "
                 "nmax_ps sl_whole sl_rest m_rest md_ready msg_last absent_ok cand_ok qmax_ok mnew_ok m_ready m_kept mexp_ps arg_ready p_ready c_ready msg_ready seg_ps acc_scaled acc_done passed").split()
        S = {n: sem(n) for n in names}
        kv_in = [sem(f"kv_in{s}") for s in range(R)]
        FIRST, LEAD, LAG = 7, 4, 4
        TURNS = (NQ - LEAD - FIRST) // R

        def steps(eng, step, reads=None):
            engine = eng.engine
            for i in range(-LEAD, FIRST):
                step(i, i, read_blocks(engine, i, reads), 0, None, None)
            if reads:
                k0, n = reads
                regs = [eng.alloc_register(f"blocks{k}") for k in range(n)]
                eng.load(regs, trow[0:1, FIRST + k0:FIRST + k0 + n])
            with eng.Fori(0, TURNS) as turn:
                i = eng.snap(turn * R + FIRST)
                ts = {k0 + k: eng.snap(r, min_val=0, max_val=NT - 1) for k, r in enumerate(regs)} if reads else {}
                for s in range(R):
                    ahead = (lambda: eng.load(regs, trow[0:1, bass.ds(i + (R + k0), n)])) if reads and s == R - 2 else None
                    step(i + s, FIRST + s, ts, s, turn, ahead)
            for i in range(FIRST + R * TURNS, NQ + LAG):
                step(i, i, read_blocks(engine, i, reads), 0, None, None)

        def has(i, k):
            return not isinstance(i, int) or 0 <= i + k < NQ

        def read_blocks(engine, i, reads):
            ks = [k for k in range(reads[0], reads[0] + reads[1] - R + 1) if 0 <= i + k < NQ] if reads else []
            if not ks:
                return {}
            _, ts = nc.values_load_multi_w_load_instructions(trow[0:1, i + ks[0]:i + ks[-1] + 1], engines=[engine], min_val=0, max_val=NT - 1)
            return dict(zip(ks, ts))

        with nc.Block() as block:
            @block.gpsimd
            def _(pool):
                def gather(q, s, js):
                    for j in js:
                        nc.gpsimd.indirect_dma_start(
                            kv[:, s % R, j, :], None, kv_dram[:, :],
                            bass.IndirectOffsetOnAxis(ap=idx[:, s % R, j:j + 1], axis=0)).then_inc(kv_in[s % R], 16)

                def step(i, s, ts, off, turn, ahead):
                    if has(i, 2):
                        hold(pool, S["idx_ready"], i + 3, S["passed"])
                        hold(pool, S["msg_ready"], i + 3 - R, S["passed"])
                        hold(pool, S["msg_last"], i + 3 - R, S["passed"])
                        gather(i + 2, s + 2, (0, 1))
                    if has(i, -3):
                        pool.wait_ge(S["p_ready"], i - 2)
                        nc.gpsimd.tensor_tensor(msg[:, (s - 3) % 2, J - 1, :, 0:HD], kv[:, (s - 3) % R, J - 1, D:2 * D].rearrange("p (h c) -> p h c", h=H),
                                                msg[:, (s - 3) % 2, J - 1, :, HD:HC].to_broadcast([P, H, HD]), ALU.mult).then_inc(S["msg_last"], 1)
                    if has(i, -2):
                        pool.wait_ge(S["mnew_ok"], i - 1)
                        nc.gpsimd.tensor_tensor(md[:, s % 2, :], mx[:, bass.ds(ts[off - 2], 1), :].rearrange("p a h -> p (a h)"), mnew[:, s % 2, 0, :],
                                                ALU.subtract).then_inc(S["md_ready"], 1)
                    if ahead:
                        ahead()
                    if has(i, 2):
                        gather(i + 2, s + 2, (2, 3))
                steps(pool, step, (-2, R))

            @block.scalar
            def _(act):
                def columns(q, s):
                    s = s % R
                    ent = TAB[:, bass.ds(q, 1), :]
                    nc.scalar.copy(idx[:, s, :], IDX[:, bass.ds(q, 1), :].rearrange("p a n -> p (a n)")).then_inc(S["idx_ready"], 1)
                    nc.scalar.copy(cols[:, s, :], ent[:, :, 0:2 * J].rearrange("p a n -> p (a n)"))
                    nc.scalar.copy(last9[:, s, :, H:H + 1], ent[:, :, J:2 * J].rearrange("p a n -> p n a"))
                    nc.scalar.copy(brkb[:, s], ent[:, :, 2 * J:3 * J].rearrange("p a n -> p n a").to_broadcast([P, J, H])).then_inc(S["cols_ready"], 1)

                def onehot(q, s):
                    s = s % R
                    act.wait_ge(S["cols_ready"], q + 1)
                    wait(act, S["seg_ps"], q - R + 1)
                    for j in range(J):
                        last = nc.scalar.activation(oh[:, s, j, :], iota_row[:], ACT.Square, bias=cols[:, s, j:j + 1], scale=-1.0)
                    last.then_inc(S["sq_ready"], 1)
                    act.wait_ge(S["sq_ready"], q + 1)
                    nc.scalar.activation(oh[:, s], oh[:, s], ACT.Relu, bias=1.0, scale=-1.0).then_inc(S["oh_ready"], 1)

                def step(i, s, ts, off, turn, ahead):
                    if has(i, 0):
                        act.wait_ge(S["mask_ps"], i + 1)
                        wait(act, S["scan_done"], i - 1)
                        nc.scalar.copy(msk[:, s % 2, :], sMK).then_inc(S["mask_sb"], 1)
                    if has(i, 1):
                        act.wait_ge(S["oht_ps"], i + 2)
                        wait(act, S["mexp_ps"], i + 2 - R)
                        nc.scalar.copy(ohT[:, (s + 1) % R], psHT[:].rearrange("p (j n) -> p j n", j=J)).then_inc(S["oht_sb"], 1)
                    if has(i, -4):
                        act.wait_ge(S["c_ready"], i - 3)
                        wait(act, S["acc_done"], i - 4)
                        for h in range(H):
                            part = acc[:, bass.ds(ts[off - 4], 1), h, :].rearrange("p a c -> p (a c)")
                            last = nc.scalar.activation(part, part, ACT.Copy, scale=cf[:, (s - 4) % R, h:h + 1])
                        last.then_inc(S["acc_scaled"], 1)
                    if has(i, 2):
                        onehot(i + 2, s + 2)
                    if has(i, -2):
                        act.wait_ge(S["md_ready"], i - 1)
                        nc.scalar.activation(cf[:, (s - 2) % R, :], md[:, s % 2, :], ACT.Exp, scale=SCALE).then_inc(S["c_ready"], 1)
                        nc.scalar.copy(mx[:, bass.ds(ts[off - 2], 1), :].rearrange("p a h -> p (a h)"), mnew[:, s % 2, 0, :]).then_inc(S["m_kept"], 1)
                    if ahead:
                        ahead()
                    if has(i, 4):
                        wait(act, S["nmax_ps"], i - 1)
                        columns(i + 4, s + 4)
                    if has(i, -2):
                        act.wait_ge(S["arg_ready"], i - 1)
                        wait(act, S["seg_ps"], i - 3)
                        nc.scalar.activation(msg[:, s % 2, :, :, HD:HC], arg[:, s % 2, :].rearrange("p (j h a) -> p j h a", j=J, a=1),
                                             ACT.Exp, scale=SCALE).then_inc(S["p_ready"], 1)
                steps(act, step, (-4, R + 2))

            @block.tensor
            def _(pe):
                def expand_q(q, s, t, half):
                    if half == 0:
                        pe.wait_ge(S["oht_sb"], q + 1)
                    wait(pe, S["prod_half"], 2 * q - 1 + half)
                    for j in (2 * half, 2 * half + 1):
                        last = nc.tensor.matmul(psQ[:, j * D:(j + 1) * D], ohT[:, s % R, j, :],
                                                Qs[:, bass.ds(t, 1), :].rearrange("p a n -> p (a n)"), start=True, stop=True)
                    last.then_inc(S["q_half"], 1)

                def step(i, s, ts, off, turn, ahead):
                    t = ts.get(off + 1)
                    if has(i, 0):
                        pe.wait_ge(S["cols_ready"], i + 1)
                        wait(pe, S["mask_sb"], i)
                        nc.tensor.transpose(sMK, brkb[:, s % R].rearrange("p j h -> p (j h)"), top(ident[:])).then_inc(S["mask_ps"], 1)
                    if has(i, 1):
                        pe.wait_ge(S["oh_ready"], i + 2)
                        wait(pe, S["oht_sb"], i + 1)
                        for j in range(J):
                            last = nc.tensor.transpose(psHT[:, j * P:(j + 1) * P], top(oh[:, (s + 1) % R, j, :]), top(ident[:]))
                        last.then_inc(S["oht_ps"], 1)
                    if has(i, -4):
                        pe.wait_ge(S["msg_ready"], i - 3)
                        pe.wait_ge(S["msg_last"], i - 3)
                        wait(pe, S["acc_done"], i - 5)
                        for j in range(J):
                            last = nc.tensor.matmul(psO[:, s % 2, 0:H * HC], oh[:, (s - 4) % R, j, :], msg[:, s % 2, j].rearrange("p h c -> p (h c)"),
                                                    start=j == 0, stop=j == J - 1)
                        last.then_inc(S["seg_ps"], 1)
                    if ahead:
                        ahead()
                    if has(i, -1):
                        hold(pe, S["scan_done"], i, S["passed"])
                        hold(pe, S["cand_ok"], i - 1, S["passed"])
                        nc.tensor.transpose(sST, run[:, (s - 1) % 2, :], ident[0:J * H, 0:J * H]).then_inc(S["st_ps"], 1)
                    if has(i, 1):
                        expand_q(i + 1, s + 1, t, 0)
                    if has(i, -2):
                        pe.wait_ge(S["m_ready"], i - 1)
                        wait(pe, S["arg_ready"], i - 2)
                        for j in range(J):
                            for k in range(3):
                                last = nc.tensor.matmul(sME[:, j * H:(j + 1) * H], top(ohT[:, (s - 2) % R, j, :]), top(mnew[:, s % 2, k, :]), start=k == 0, stop=k == 2)
                        last.then_inc(S["mexp_ps"], 1)
                    if has(i, -1):
                        pe.wait_ge(S["sl_ready"], i)
                        for j in range(J):
                            for k, part in enumerate((last9[:, (s - 1) % R, j, :], rest9[:, (s - 1) % 2, 0, j, :], rest9[:, (s - 1) % 2, 1, j, :])):
                                last = nc.tensor.matmul(sNM[:, j * (H + 1):(j + 1) * (H + 1)], top(oh[:, (s - 1) % R, j, :]), top(part), start=k == 0, stop=k == 2)
                        last.then_inc(S["nmax_ps"], 1)
                    if has(i, 0):
                        pe.wait_ge(S["l_ready"], 2 * i + 2)
                        wait(pe, S["arg_ready"], i - 1)
                        nc.tensor.transpose(sLT, lg[:, s % 3, :], ident[:]).then_inc(S["lt_ps"], 1)
                    if has(i, 1):
                        expand_q(i + 1, s + 1, t, 1)
                steps(pe, step, (1, R))

            @block.vector
            def _(dve):
                def logits_half(i, s, turn, half):
                    dve.wait_ge(S["q_half"], i * 2 + 1 + half)
                    if half == 0:
                        before = (s // R + 1) * J * 16
                        dve.wait_ge(kv_in[s % R], before if turn is None else turn * (J * 16) + before)
                    wait(dve, S["l_ready"], 2 * i - 1 + half)
                    cs, js = slice(2 * half * D, (2 * half + 2) * D), slice(2 * half, 2 * half + 2)
                    nc.vector.tensor_tensor(prod[:, cs].rearrange("p (j n) -> p j n", j=2), psQ[:, cs].rearrange("p (j n) -> p j n", j=2),
                                            kv[:, s % R, js, 0:D], ALU.mult).then_inc(S["prod_half"], 1)

                def sum_half(i, s, half):
                    dve.wait_ge(S["prod_half"], i * 2 + 1 + half)
                    cs, gs = slice(2 * half * D, (2 * half + 2) * D), slice(2 * half * H, (2 * half + 2) * H)
                    nc.vector.tensor_reduce(lg[:, s % 3, gs], prod[:, cs].rearrange("p (g c) -> p g c", c=HD), AX.X, ALU.add).then_inc(S["l_ready"], 1)

                def bc(ap, n):
                    return ap.rearrange("p (a o) -> p a o", o=1).to_broadcast([P, ap.shape[1], n])

                def step(i, s, ts, off, turn, ahead):
                    now, runs, maxima, msgs, sums = has(i, 0), has(i, -1), has(i, -2), has(i, -3), has(i, -4)
                    s1, s2 = s - 1, s - 2
                    if maxima:
                        mcur = mx[:, bass.ds(ts[off - 2], 1), :].rearrange("p a h -> p (a h)")
                        m = mnew[:, s2 % 2]
                        nm = sNM.rearrange("p (j h) -> p j h", j=J)
                    if now:
                        logits_half(i, s, turn, 0)
                    if maxima:
                        dve.wait_ge(S["nmax_ps"], i - 1)
                        nc.vector.tensor_scalar(absent[:].rearrange("p (j a) -> p j a", a=1), nm[:, :, H:H + 1], BIG, -BIG, ALU.mult, ALU.add).then_inc(S["absent_ok"], 1)
                    if runs:
                        dve.wait_ge(S["lt_ps"], i)
                        dve.wait_ge(S["mask_sb"], i)
                        nc.vector.tensor_tensor_scan(run[:, s1 % 2, :], msk[:, s1 % 2, :], sLT, -BIG, ALU.add, ALU.max).then_inc(S["scan_done"], 1)
                    if maxima:
                        dve.wait_ge(S["absent_ok"], i - 1)
                        nc.vector.tensor_tensor(cand[:], nm[:, :, 0:H], bc(absent[:], H), ALU.add).then_inc(S["cand_ok"], 1)
                    if now:
                        logits_half(i, s, turn, 1)
                    if maxima:
                        dve.wait_ge(S["cand_ok"], i - 1)
                        nc.vector.tensor_reduce(qmax[:], cand[:].rearrange("p j h -> p h j"), AX.X, ALU.max).then_inc(S["qmax_ok"], 1)
                    if now:
                        sum_half(i, s, 0)
                    if maxima:
                        dve.wait_ge(S["qmax_ok"], i - 1)
                        wait(dve, S["m_kept"], i - 2)
                        nc.vector.tensor_tensor(m[:, 0, :], mcur, qmax[:], ALU.max).then_inc(S["mnew_ok"], 1)
                    if now:
                        sum_half(i, s, 1)
                    if ahead:
                        ahead()
                    if maxima:
                        dve.wait_ge(S["mnew_ok"], i - 1)
                        nc.vector.tensor_tensor(m[:, 1, :], m[:, 0, :], top(m[:, 0, :]), ALU.subtract).then_inc(S["m_rest"], 1)
                    if runs:
                        dve.wait_ge(S["st_ps"], i)
                        nc.vector.tensor_tensor(last9[:, s1 % R, :, 0:H], sST.rearrange("p (j h) -> p j h", j=J), bc(cols[:, s1 % R, J:2 * J], H), ALU.mult).then_inc(S["sl_whole"], 1)
                    if maxima:
                        dve.wait_ge(S["m_rest"], i - 1)
                        nc.vector.tensor_tensor(m[:, 2, :], m[:, 1, :], top(m[:, 1, :]), ALU.subtract).then_inc(S["m_ready"], 1)
                    if runs:
                        dve.wait_ge(S["sl_whole"], i)
                        nc.vector.tensor_tensor(rest9[:, s1 % 2, 0], last9[:, s1 % R], top(last9[:, s1 % R]), ALU.subtract).then_inc(S["sl_rest"], 1)
                    if sums:
                        ac = acc[:, bass.ds(ts[off - 4], 1)].rearrange("p a h c -> p (a h) c")
                        dve.wait_ge(S["acc_scaled"], i - 3)
                        dve.wait_ge(S["seg_ps"], i - 3)
                        nc.vector.tensor_tensor(ac, ac, psO[:, s % 2, 0:H * HC].rearrange("p (h c) -> p h c", h=H), ALU.add).then_inc(S["acc_done"], 1)
                    if runs:
                        dve.wait_ge(S["sl_rest"], i)
                        nc.vector.tensor_tensor(rest9[:, s1 % 2, 1], rest9[:, s1 % 2, 0], top(rest9[:, s1 % 2, 0]), ALU.subtract).then_inc(S["sl_ready"], 1)
                    if maxima:
                        dve.wait_ge(S["mexp_ps"], i - 1)
                        nc.vector.tensor_tensor(arg[:, s % 2, :], lg[:, s2 % 3, :], sME, ALU.subtract).then_inc(S["arg_ready"], 1)
                    if msgs:
                        dve.wait_ge(S["p_ready"], i - 2)
                        nc.vector.tensor_tensor(msg[:, (s - 3) % 2, 0:J - 1, :, 0:HD], kv[:, (s - 3) % R, 0:J - 1, D:2 * D].rearrange("p j (h c) -> p j h c", h=H),
                                                msg[:, (s - 3) % 2, 0:J - 1, :, HD:HC].to_broadcast([P, J - 1, H, HD]), ALU.mult).then_inc(S["msg_ready"], 1)

                steps(dve, step, (-4, R + 2))
                dve.wait_ge(S["acc_done"], NQ)


def nodes(nc, x, w, out, acc, ident):
    with ExitStack() as ctx:
        sb = lambda n, s, d=F32: ctx.enter_context(nc.sbuf_tensor(n, s, d))
        ps = lambda n, s: ctx.enter_context(nc.psum_tensor(n, s, F32))
        sem = lambda n: ctx.enter_context(nc.semaphore(n))
        R, FIRST, LAG = 6, 7, 5
        TURNS = (NT - FIRST) // R
        assert (NT - FIRST) % R == 0
        wsk = sb("wsk", [P, KC, D])
        wo = sb("wo", [P, KC, D])
        w1 = sb("w1", [P, KC, FF])
        w2 = sb("w2", [P, FC, D])
        rows = {n: sb(f"r_{n}", [P, D]) for n in ("bskip", "bo", "b2", "g1", "be1", "g2", "be2")}
        b1c = sb("b1c", [P, FC])
        xin = sb("nx", [P, R, D])
        xT = sb("nxT", [P, KC * P])
        saT = sb("saT", [P, KC * P])
        x1T = sb("x1T", [P, KC * P])
        den = sb("den", [P, H])
        att = sb("att", [P, D])
        sa = sb("sa", [P, 2, D])
        xb = sb("xb", [P, 2, D])
        y = sb("y", [P, D])
        y2 = sb("y2", [P, D])
        x1 = sb("x1", [P, 2, D])
        x1b = sb("x1b", [P, R, D])
        hT = sb("hT", [P, 2, FC, P])
        z = sb("z", [P, D])
        zz = sb("zz", [P, 2, D])
        st = sb("st", [P, 3, 6])
        ag = sb("ag", [P, 3, 2])
        sd = sb("sd", [P, 3, 1])
        rs = sb("rs", [P, 3, 1])
        ob = sb("ob", [P, 2, D])
        eps = sb("eps", [P, 1])
        pX = ps("pX", [P, 512])
        pA = ps("pA", [P, 512])
        pC = ps("pC", [P, 512])
        pS = ps("pS", [P, 512])
        pB = ps("pB", [P, 512])
        pH = ps("pH", [P, 2, 512])
        pF = ps("pF", [P, 512])
        wsk_in = sem("wsk_in")
        wo_in = sem("wo_in")
        w1_in = sem("w1_in")
        w2_in = sem("w2_in")
        b1_in = sem("b1_in")
        rows_in = sem("brows_in")
        x_in = [sem(f"nx_in{s}") for s in range(R)]
        out_done = [sem(f"out_done{s}") for s in range(2)]
        names = ("xt_ps xt_sb skip_ps sa_ready sat_ps sat_sb wo_ps x1_ready x1t_ps x1t_sb h_ps h_sb f_ps xb_ready x1b_ready n1_ready n2_ready zz_ready "
                 "y_read z_read o_ready p1 pv den1 den2 att1 att2 bn0 bn1 bn2 rs0 rs1 rs2 eps_ok passed stat0 stat1 stat2 root0 root1 root2").split()
        S = {n: sem("n_" + n) for n in names}

        def steps(eng, step):
            for i in range(0, FIRST):
                step(i, i, None)
            with eng.Fori(0, TURNS) as turn:
                i = eng.snap(turn * R + FIRST)
                for s in range(R):
                    step(i + s, FIRST + s, turn)
            for i in range(NT, NT + LAG):
                step(i, i, None)

        def has(i, k):
            return not isinstance(i, int) or 0 <= i + k < NT

        def first(i, k):
            return isinstance(i, int) and i + k == 0

        with nc.Block() as block:
            @block.sync
            def _(sp):
                def load(t, s, r=P):
                    wait(sp, S["zz_ready"], t - R + 1)
                    sp.dma_start(xin[0:r, s % R, :], x[bass.ds(t * P, r), :]).then_inc(x_in[s % R], 16)
                for t in range(R):
                    load(t, t)
                    if t == 0:
                        sp.dma_start(wsk[:], w["Wskip"].rearrange("(c p) n -> p c n", p=P)).then_inc(wsk_in, 16)
                        sp.dma_start(wo[:], w["Wo"].rearrange("(c p) n -> p c n", p=P)).then_inc(wo_in, 16)
                with sp.Fori(R, NT - R, R) as i:
                    for s in range(R):
                        load(i + s, s)
                load(NT - 1, NT - 1, TAIL)
                assert NT % R == 1

            @block.tensor
            def _(pe):
                def turn_over(dst, src_, done):
                    for c in range(KC):
                        last = nc.tensor.transpose(dst[:, c * P:(c + 1) * P], src_[:, c * P:(c + 1) * P], ident[:])
                    last.then_inc(done, 1)

                def step(i, s, turn):
                    if has(i, 0):
                        pe.wait_ge(x_in[s % R], (s // R + 1) * 16 if turn is None else turn * 16 + (s // R + 1) * 16)
                        turn_over(pX, xin[:, s % R, :], S["xt_ps"])
                    if has(i, -1):
                        pe.wait_ge(S["sa_ready"], i)
                        turn_over(pA, sa[:, (s - 1) % 2, :], S["sat_ps"])
                    if has(i, -2):
                        pe.wait_ge(S["x1_ready"], i - 1)
                        turn_over(pC, x1[:, s % 2, :], S["x1t_ps"])
                    if has(i, 0):
                        pe.wait_ge(S["xt_sb"], i + 1)
                        if first(i, 0):
                            pe.wait_ge(wsk_in, 16)
                        wait(pe, S["sa_ready"], i)
                        for c in range(KC):
                            last = nc.tensor.matmul(pS[:, 0:D], xT[:, c * P:(c + 1) * P], wsk[:, c, :], start=c == 0, stop=c == KC - 1)
                        last.then_inc(S["skip_ps"], 1)
                    if has(i, -1):
                        pe.wait_ge(S["sat_sb"], i)
                        if first(i, -1):
                            pe.wait_ge(wo_in, 16)
                        wait(pe, S["y_read"], i - 1)
                        for c in range(KC):
                            last = nc.tensor.matmul(pB[:, 0:D], saT[:, c * P:(c + 1) * P], wo[:, c, :], start=c == 0, stop=c == KC - 1)
                        last.then_inc(S["wo_ps"], 1)
                    if has(i, -2):
                        pe.wait_ge(S["x1t_sb"], i - 1)
                        if first(i, -2):
                            pe.wait_ge(w1_in, 16)
                        for f in range(FC):
                            if f % 4 == 0:
                                wait(pe, S["h_sb"], (i - 3) * 2 + f // 4 + 1 if has(i, -3) else 0)
                            for c in range(KC):
                                last = nc.tensor.matmul(pH[:, f // 4, (f % 4) * P:(f % 4 + 1) * P], w1[:, c, f * P:(f + 1) * P], x1T[:, c * P:(c + 1) * P],
                                                        start=c == 0, stop=c == KC - 1)
                            if f % 4 == 3:
                                last.then_inc(S["h_ps"], 1)
                    if has(i, -3):
                        pe.wait_ge(S["h_sb"], (i - 3) * 2 + 2)
                        if first(i, -3):
                            pe.wait_ge(w2_in, 16)
                        wait(pe, S["z_read"], i - 3)
                        for f in range(FC):
                            last = nc.tensor.matmul(pF[:, 0:D], hT[:, (s - 3) % 2, f, :], w2[:, f, :], start=f == 0, stop=f == FC - 1)
                        last.then_inc(S["f_ps"], 1)
                steps(pe, step)

            @block.scalar
            def _(act):
                for n, t in rows.items():
                    act.dma_start(t[:], row_bcast(w[n], D)).then_inc(rows_in, 16)
                with nc.allow_non_contiguous_dma("a bias by partitions"):
                    act.dma_start(b1c[:], w["b1"].rearrange("(c p) -> p c", p=P)).then_inc(b1_in, 16)
                act.wait_ge(S["eps_ok"], 1)
                act.wait_ge(b1_in, 16)

                def root(k, t):
                    act.wait_ge(S[f"stat{k}"], t + 1)
                    nc.scalar.activation(sd[:, k, :], ag[:, k, 1:2], ACT.Sqrt, bias=eps[:]).then_inc(S[f"root{k}"], 1)

                def relu(i, s, bank):
                    act.wait_ge(S["h_ps"], (i - 2) * 2 + bank + 1)
                    if bank == 0:
                        wait(act, S["f_ps"], i - 3)
                    for f in range(4 * bank, 4 * bank + 4):
                        last = nc.scalar.activation(hT[:, s % 2, f, :], pH[:, bank, (f % 4) * P:(f % 4 + 1) * P], ACT.Relu, bias=b1c[:, f:f + 1])
                    last.then_inc(S["h_sb"], 1)

                def step(i, s, turn):
                    if has(i, 0):
                        act.wait_ge(S["xt_ps"], i + 1)
                        wait(act, S["skip_ps"], i)
                        nc.scalar.copy(xT[:], pX[:, 0:KC * P]).then_inc(S["xt_sb"], 1)
                    if has(i, -1):
                        act.wait_ge(S["sat_ps"], i)
                        wait(act, S["wo_ps"], i - 1)
                        nc.scalar.copy(saT[:], pA[:, 0:KC * P]).then_inc(S["sat_sb"], 1)
                    if has(i, -2):
                        act.wait_ge(S["x1t_ps"], i - 1)
                        wait(act, S["h_ps"], (i - 3) * 2 + 2 if has(i, -3) else 0)
                        nc.scalar.copy(x1T[:], pC[:, 0:KC * P]).then_inc(S["x1t_sb"], 1)
                    if has(i, -5):
                        root(2, i - 5)
                    if has(i, -4):
                        root(1, i - 4)
                    if has(i, -2):
                        relu(i, s, 0)
                    if has(i, -1):
                        root(0, i - 1)
                    if has(i, -2):
                        relu(i, s, 1)
                steps(act, step)

            @block.gpsimd
            def _(pool):
                def step(i, s, turn):
                    if has(i, 0):
                        pool.wait_ge(x_in[s % R], (s // R + 1) * 16 if turn is None else turn * 16 + (s // R + 1) * 16)
                        wait(pool, S["y_read"], i - 1)
                        nc.gpsimd.tensor_tensor(xb[:, s % 2, :], xin[:, s % R, :], rows["bo"][:], ALU.add).then_inc(S["xb_ready"], 1)
                    if has(i, -4):
                        t = i - 4
                        pool.wait_ge(S["n2_ready"], t + 1)
                        nc.gpsimd.tensor_tensor(z[:], z[:], rows["g2"][:], ALU.mult).then_inc(S["pv"], 1)
                        pool.wait_ge(S["pv"], (i - 4) * 2 + 1)
                        nc.gpsimd.tensor_tensor(z[:], z[:], rows["be2"][:], ALU.add).then_inc(S["pv"], 1)
                        pool.wait_ge(S["pv"], (i - 4) * 2 + 2)
                        wait(pool, S["o_ready"], t - 1)
                        nc.gpsimd.tensor_tensor(zz[:, s % 2, :], z[:], xin[:, (s - 4) % R, :], ALU.add).then_inc(S["zz_ready"], 1)
                    if has(i, -1):
                        t = i - 1
                        pool.wait_ge(S["n1_ready"], i)
                        nc.gpsimd.tensor_tensor(y2[:], y2[:], rows["g1"][:], ALU.mult).then_inc(S["p1"], 1)
                        pool.wait_ge(S["p1"], i)
                        wait(pool, S["x1t_ps"], i - 2)
                        nc.gpsimd.tensor_tensor(x1[:, (s - 1) % 2, :], y2[:], rows["be1"][:], ALU.add).then_inc(S["x1_ready"], 1)
                        pool.wait_ge(S["x1_ready"], i)
                        wait(pool, S["z_read"], i - R)
                        nc.gpsimd.tensor_tensor(x1b[:, (s - 1) % R, :], x1[:, (s - 1) % 2, :], rows["b2"][:], ALU.add).then_inc(S["x1b_ready"], 1)
                    if has(i, -5):
                        store(i - 5, s - 5, P)

                def store(t, s, r):
                    pool.wait_ge(S["o_ready"], t + 1)
                    if isinstance(t, int) and t == NT - 1:
                        r = TAIL
                    pool.dma_start(out[bass.ds(t * P, r), :], ob[0:r, s % 2, :]).then_inc(out_done[s % 2], 16)
                pool.dma_start(w1[:], w["W1"].rearrange("(c p) n -> p c n", p=P)).then_inc(w1_in, 16)
                pool.dma_start(w2[:], w["W2"].rearrange("(c p) n -> p c n", p=P)).then_inc(w2_in, 16)
                pool.wait_ge(rows_in, len(rows) * 16)
                steps(pool, step)
                pool.wait_ge(out_done[0], 16 * len(range(0, NT, 2)))
                pool.wait_ge(out_done[1], 16 * len(range(1, NT, 2)))

            @block.vector
            def _(dve):
                nc.vector.memset(eps[:], 1e-5).then_inc(S["eps_ok"], 1)
                dve.wait_ge(rows_in, len(rows) * 16)

                def stats(k, t, in_):
                    nc.vector.bn_stats(st[:, k, :], in_).then_inc(S[f"bn{k}"], 1)
                    hold(dve, S[f"bn{k}"], t + 1, S["passed"])
                    nc.vector.bn_aggr(ag[:, k, :], st[:, k, :]).then_inc(S[f"stat{k}"], 1)

                def normed(k, t, out_, in_):
                    dve.wait_ge(S[f"root{k}"], t + 1)
                    nc.vector.reciprocal(rs[:, k, :], sd[:, k, :]).then_inc(S[f"rs{k}"], 1)
                    dve.wait_ge(S[f"rs{k}"], t + 1)
                    return nc.vector.tensor_scalar(out_, in_, ag[:, k, 0:1], rs[:, k, 0:1], ALU.subtract, ALU.mult)

                def step(i, s, turn):
                    if has(i, -5):
                        t = i - 5
                        dve.wait_ge(S["zz_ready"], t + 1)
                        stats(2, t, zz[:, (s - 5) % 2, :])
                    if has(i, -4):
                        t = i - 4
                        dve.wait_ge(S["f_ps"], t + 1)
                        dve.wait_ge(S["x1b_ready"], t + 1)
                        wait(dve, S["zz_ready"], t)
                        nc.vector.tensor_tensor(z[:], x1b[:, (s - 4) % R, :], pF[:, 0:D], ALU.add).then_inc(S["z_read"], 1)
                        dve.wait_ge(S["z_read"], t + 1)
                        stats(1, t, z[:])
                    if has(i, -5):
                        t = i - 5
                        if turn is None:
                            wait(dve, out_done[(s - 5) % 2], (t // 2) * 16)
                        else:
                            dve.wait_ge(out_done[(s - 5) % 2], turn * (R // 2 * 16) + ((s - 5) // 2) * 16)
                        n = normed(2, t, ob[:, (s - 5) % 2, :], zz[:, (s - 5) % 2, :])
                        n.then_inc(S["o_ready"], 1)
                    if has(i, 0):
                        ac = acc[:, bass.ds(i, 1)].rearrange("p a h c -> p (a h) c")
                        nc.vector.tensor_scalar(den[:].rearrange("p (h a) -> p h a", a=1), ac[:, :, HD:HC], 1e-16, None, ALU.add).then_inc(S["den1"], 1)
                        dve.wait_ge(S["den1"], i + 1)
                        nc.vector.reciprocal(den[:], den[:]).then_inc(S["den2"], 1)
                    if has(i, -4):
                        normed(1, i - 4, z[:], z[:]).then_inc(S["n2_ready"], 1)
                    if has(i, 0):
                        dve.wait_ge(S["den2"], i + 1)
                        nc.vector.tensor_tensor(att[:].rearrange("p (h c) -> p h c", h=H), ac[:, :, 0:HD],
                                                den[:].rearrange("p (h a) -> p h a", a=1).to_broadcast([P, H, HD]), ALU.mult).then_inc(S["att1"], 1)
                        dve.wait_ge(S["att1"], i + 1)
                        nc.vector.tensor_tensor(att[:], att[:], rows["bskip"][:], ALU.add).then_inc(S["att2"], 1)
                        dve.wait_ge(S["att2"], i + 1)
                        dve.wait_ge(S["skip_ps"], i + 1)
                        wait(dve, S["sat_ps"], i - 1)
                        nc.vector.tensor_tensor(sa[:, s % 2, :], att[:], pS[:, 0:D], ALU.add).then_inc(S["sa_ready"], 1)
                    if has(i, -1):
                        t = i - 1
                        dve.wait_ge(S["wo_ps"], i)
                        dve.wait_ge(S["xb_ready"], i)
                        nc.vector.tensor_tensor(y[:], xb[:, (s - 1) % 2, :], pB[:, 0:D], ALU.add).then_inc(S["y_read"], 1)
                        dve.wait_ge(S["y_read"], i)
                        stats(0, t, y[:])
                        wait(dve, S["x1_ready"], i - 1)
                        normed(0, t, y2[:], y[:]).then_inc(S["n1_ready"], 1)
                steps(dve, step)


def gnn_program(nc, x, src, dst, w, out):
    kv_dram = nc.dram_tensor("kv_table", (N, 2 * D), F32, kind="Internal").ap()
    srcp = nc.dram_tensor("src_padded", (EP,), I32, kind="Internal").ap()
    dstp = nc.dram_tensor("dst_padded", (EP,), I32, kind="Internal").ap()
    descents_dram = nc.dram_tensor("descent_table", (TE,), F32, kind="Internal").ap()
    counter_dram = nc.dram_tensor("node_counter", (NT * P,), I32, kind="Internal").ap()
    tq_dram = nc.dram_tensor("pair_block", (NP,), I32, kind="Internal").ap()
    with ExitStack() as ctx:
        sb = lambda n, s, d=F32: ctx.enter_context(nc.sbuf_tensor(n, s, d))
        ident = sb("ident", [P, P])
        iota_row = sb("iota_row", [P, P])
        pair_no = sb("pair_no", [P, PC])
        disorder = sb("disorder", [1, 1], I32)
        acc = sb("acc", [P, NT, H, HC])
        ready = ctx.enter_context(nc.semaphore("const_ready"))
        with ExitStack() as c2:
            sb2 = lambda n, s, d=F32: c2.enter_context(nc.sbuf_tensor(n, s, d))
            Qs = sb2("Qs", [P, NT, D])
            mx = sb2("mx", [P, NT, H])
            TAB = sb2("TAB", [P, NQ, NTAB], BF16)
            IDX = sb2("IDX", [P, NQ, J], I16)
            trow = sb2("trow", [1, NQ + 8], I32)
            with nc.Block() as block:
                @block.gpsimd
                def _(pool):
                    nc.gpsimd.memset(ident[:], 0.0).then_inc(ready, 1)
                    pool.wait_ge(ready, 1)
                    nc.gpsimd.affine_select(ident[:], ident[:], [[-1, P]], ALU.not_equal, 1.0, base=0, channel_multiplier=1).then_inc(ready, 1)
                    nc.gpsimd.iota(iota_row[:], [[1, P]], base=0, channel_multiplier=0, allow_small_or_imprecise_dtypes=True)
                    nc.gpsimd.iota(pair_no[:], [[P, PC]], base=0, channel_multiplier=1, allow_small_or_imprecise_dtypes=True)
            project(nc, x, w, kv_dram, Qs, ident, ready, src, dst, srcp, dstp, descents_dram, disorder, acc, mx)
            sort_edges(nc, src, dst, srcp, dstp, counter_dram, iota_row, pair_no, disorder)
            plan(nc, srcp, dstp, tq_dram, TAB, IDX, trow, ident, pair_no)
            edges(nc, kv_dram, Qs, acc, mx, TAB, IDX, trow, ident, iota_row)
        nodes(nc, x, w, out, acc, ident)


_W = ["Wq", "bq", "Wk", "bk", "Wv", "bv", "Wskip", "bskip", "Wo", "bo", "W1", "b1", "W2", "b2", "g1", "be1", "g2", "be2"]


def kernel(**inputs):
    import numpy as _np
    import concourse.bacc as _bacc
    from concourse import mybir as _mybir
    from concourse.bass_utils import run_bass_kernel_spmd as _run

    nc = _bacc.Bacc("TRN2", target_bir_lowering=False, num_devices=1)
    arrays, aps = {}, {}
    for name in ["x", "src", "dst"] + ["L0_gnn_" + n for n in _W]:
        a = _np.ascontiguousarray(inputs[name])
        arrays["in_" + name] = a
        aps[name] = nc.dram_tensor("in_" + name, a.shape, _mybir.dt.from_np(a.dtype), kind="ExternalInput").ap()
    out = nc.dram_tensor("out", (N, D), F32, kind="ExternalOutput").ap()
    gnn_program(nc, aps["x"], aps["src"], aps["dst"], {n: aps["L0_gnn_" + n] for n in _W}, out)
    r = _run(nc, [arrays], core_ids=[0])
    return r.results[0]["out"]
```
